# Optimizing a Trainium2 kernel written in Bass

```python
import numpy as np
import jax
import jax.numpy as jnp

def _softmax(x, axis=-1):
    return jax.nn.softmax(x, axis=axis)

def _gelu(x):
    return jax.nn.gelu(x, approximate=True)

def _silu(x):
    return jax.nn.silu(x)

def _sigmoid(x):
    return jax.nn.sigmoid(x)

def _layernorm(x, axis=-1, eps=1e-05):
    m = jnp.mean(x, axis=axis, keepdims=True)
    v = jnp.var(x, axis=axis, keepdims=True)
    return (x - m) / jnp.sqrt(v + eps)

def _scatter_add(tgt, idx, src, axis=0):
    return tgt.at[idx].add(src)

def _segment_sum(src, seg, n):
    return jax.ops.segment_sum(src, seg, n)
kernel_name = 'mk_xattn_ffn_d1_seqx_r8_b32f87'

def setup_inputs(seed: int=0):
    np.random.seed(seed)
    _w = jnp.asarray

    def _rec_inputs():
        import jax
        import jax.numpy as jnp
        _rk = jax.random.key(seed)
        x = 0.000341 + 1 * jax.random.normal(jax.random.fold_in(_rk, 1), (16, 128, 256), jnp.float32)
        _lenS = 128 - jax.random.randint(jax.random.fold_in(_rk, 7), (16,), 0, max(1, 128 // 4) + 1, jnp.int32)
        _lenS2 = 128 - jax.random.randint(jax.random.fold_in(_rk, 8), (16,), 0, max(1, 128 // 4) + 1, jnp.int32)
        _ctx_2048P = jax.random.normal(jax.random.fold_in(_rk, 11), (16, 16, 256), jnp.float32)
        _ctx_2048c = jax.random.dirichlet(jax.random.fold_in(_rk, 511), 0.3 * jnp.ones((16,), jnp.float32), (16, 128))
        _ctx_2048t = jnp.einsum('bsk,bkd->bsd', _ctx_2048c, _ctx_2048P)
        _ctx_2048t = _ctx_2048t * jax.lax.rsqrt(jnp.mean(jnp.square(_ctx_2048t)) + 1e-12) * 0.953939
        ctx_2048 = -1.47943e-05 + 1.00017 * (_ctx_2048t + 0.3 * jax.random.normal(jax.random.fold_in(_rk, 611), (16, 128, 256), jnp.float32))
        return (x, ctx_2048)
    x, ctx_2048 = _rec_inputs()

    def _L0_xattn_setup():
        import jax, jax.numpy as jnp
        import numpy as np

        def _wkv(time_decay, time_first, k, v):
            w = -jnp.exp(time_decay)
            u = time_first
            B, T, C = k.shape
            aa = jnp.zeros((B, C), dtype=k.dtype)
            bb = jnp.zeros((B, C), dtype=k.dtype)
            pp = jnp.full((B, C), -1e+38, dtype=k.dtype)

            def step(carry, kv_t):
                aa, bb, pp = carry
                kt, vt = kv_t
                ww = u + kt
                q = jnp.maximum(pp, ww)
                e1 = jnp.exp(pp - q)
                e2 = jnp.exp(ww - q)
                y_t = (e1 * aa + e2 * vt) / (e1 * bb + e2)
                ww2 = pp + w
                q2 = jnp.maximum(ww2, kt)
                e1b = jnp.exp(ww2 - q2)
                e2b = jnp.exp(kt - q2)
                new_carry = (e1b * aa + e2b * vt, e1b * bb + e2b, q2)
                return (new_carry, y_t)
            ks = jnp.transpose(k, (1, 0, 2))
            vs = jnp.transpose(v, (1, 0, 2))
            _, ys = jax.lax.scan(step, (aa, bb, pp), (ks, vs))
            return jnp.transpose(ys, (1, 0, 2))
        key = jax.random.key(seed)
        k1, k2, k3, k4 = jax.random.split(key, 4)
        B, T, C = (8, 128, 256)
        return {'batch_size': B, 'seq_len': T, 'embedding_dim': C, 'time_decay': jax.random.normal(k1, (C,), dtype=jnp.float32), 'time_first': jax.random.normal(k2, (C,), dtype=jnp.float32), 'k': jax.random.normal(k3, (B, T, C), dtype=jnp.float32), 'v': jax.random.normal(k4, (B, T, C), dtype=jnp.float32)}
    _L0_xattn_all = _L0_xattn_setup()
    _L0_xattn_in = {k: v for k, v in _L0_xattn_all.items() if k in ('time_decay', 'time_first')}
    del _L0_xattn_all

    def _L0_ffn_setup():
        import jax, jax.numpy as jnp
        import numpy as np
        DIM = 256
        INTER = 176
        E = 16
        TOPK = 4
        G = 4
        TOPK_G = 2
        N_SHARED = 2
        SHARED_INTER = N_SHARED * INTER
        ROUTE_SCALE = 1.0

        def _moe_forward(x, Wg, W1, W3, W2, Ws1, Ws3, Ws2):
            B, S, D = x.shape
            xt = x.reshape(-1, D)
            T = xt.shape[0]
            scores = jax.nn.softmax(xt @ Wg.T, axis=-1)
            sg = scores.reshape(T, G, E // G)
            group_scores = sg.max(axis=-1)
            gidx = jax.lax.top_k(group_scores, TOPK_G)[1]
            gmask = jax.nn.one_hot(gidx, G, dtype=jnp.float32).sum(axis=1) > 0
            masked = jnp.where(gmask[:, :, None], sg, -jnp.inf).reshape(T, E)
            topi = jax.lax.top_k(masked, TOPK)[1]
            weights = jnp.take_along_axis(scores, topi, axis=1) * ROUTE_SCALE
            combine = jnp.zeros((T, E), xt.dtype).at[jnp.arange(T)[:, None], topi].add(weights)
            h = jax.nn.silu(jnp.einsum('td,eid->eti', xt, W1)) * jnp.einsum('td,eid->eti', xt, W3)
            expert_out = jnp.einsum('eti,edi->etd', h, W2)
            y = jnp.einsum('etd,te->td', expert_out, combine)
            z = jax.nn.silu(xt @ Ws1.T) * (xt @ Ws3.T) @ Ws2.T
            return (y + z).reshape(B, S, D)
        key = jax.random.key(seed)
        ks = jax.random.split(key, 8)
        s = 0.02
        x = jax.random.normal(ks[0], (1, 256, DIM), dtype=jnp.float32)
        Wg = jax.random.normal(ks[1], (E, DIM), dtype=jnp.float32) * s
        W1 = jax.random.normal(ks[2], (E, INTER, DIM), dtype=jnp.float32) * s
        W3 = jax.random.normal(ks[3], (E, INTER, DIM), dtype=jnp.float32) * s
        W2 = jax.random.normal(ks[4], (E, DIM, INTER), dtype=jnp.float32) * s
        Ws1 = jax.random.normal(ks[5], (SHARED_INTER, DIM), dtype=jnp.float32) * s
        Ws3 = jax.random.normal(ks[6], (SHARED_INTER, DIM), dtype=jnp.float32) * s
        Ws2 = jax.random.normal(ks[7], (DIM, SHARED_INTER), dtype=jnp.float32) * s
        return {'x': x, 'Wg': Wg, 'W1': W1, 'W3': W3, 'W2': W2, 'Ws1': Ws1, 'Ws3': Ws3, 'Ws2': Ws2}
    _L0_ffn_all = _L0_ffn_setup()
    _L0_ffn_in = {k: v for k, v in _L0_ffn_all.items() if k in ('Wg', 'W1', 'W3', 'W2', 'Ws1', 'Ws3', 'Ws2')}
    del _L0_ffn_all
    return {'x': x, 'ctx_2048': ctx_2048, 'L0_xattn_time_decay': _L0_xattn_in['time_decay'], 'L0_xattn_time_first': _L0_xattn_in['time_first'], 'L0_ffn_Wg': _L0_ffn_in['Wg'], 'L0_ffn_W1': _L0_ffn_in['W1'], 'L0_ffn_W3': _L0_ffn_in['W3'], 'L0_ffn_W2': _L0_ffn_in['W2'], 'L0_ffn_Ws1': _L0_ffn_in['Ws1'], 'L0_ffn_Ws3': _L0_ffn_in['Ws3'], 'L0_ffn_Ws2': _L0_ffn_in['Ws2']}

def reference(x, ctx_2048, L0_xattn_time_decay, L0_xattn_time_first, L0_ffn_Wg, L0_ffn_W1, L0_ffn_W3, L0_ffn_W2, L0_ffn_Ws1, L0_ffn_Ws3, L0_ffn_Ws2):
    import jax
    import jax.numpy as jnp

    def _L0_xattn_ref(batch_size, seq_len, embedding_dim, time_decay, time_first, k, v):
        import jax, jax.numpy as jnp
        import numpy as np

        def _wkv(time_decay, time_first, k, v):
            w = -jnp.exp(time_decay)
            u = time_first
            B, T, C = k.shape
            aa = jnp.zeros((B, C), dtype=k.dtype)
            bb = jnp.zeros((B, C), dtype=k.dtype)
            pp = jnp.full((B, C), -1e+38, dtype=k.dtype)

            def step(carry, kv_t):
                aa, bb, pp = carry
                kt, vt = kv_t
                ww = u + kt
                q = jnp.maximum(pp, ww)
                e1 = jnp.exp(pp - q)
                e2 = jnp.exp(ww - q)
                y_t = (e1 * aa + e2 * vt) / (e1 * bb + e2)
                ww2 = pp + w
                q2 = jnp.maximum(ww2, kt)
                e1b = jnp.exp(ww2 - q2)
                e2b = jnp.exp(kt - q2)
                new_carry = (e1b * aa + e2b * vt, e1b * bb + e2b, q2)
                return (new_carry, y_t)
            ks = jnp.transpose(k, (1, 0, 2))
            vs = jnp.transpose(v, (1, 0, 2))
            _, ys = jax.lax.scan(step, (aa, bb, pp), (ks, vs))
            return jnp.transpose(ys, (1, 0, 2))
        assert seq_len <= 128
        return _wkv(time_decay, time_first, k, v)

    def _L0_ffn_ref(x, Wg, W1, W3, W2, Ws1, Ws3, Ws2):
        import jax, jax.numpy as jnp
        import numpy as np
        DIM = 256
        INTER = 176
        E = 16
        TOPK = 4
        G = 4
        TOPK_G = 2
        N_SHARED = 2
        SHARED_INTER = N_SHARED * INTER
        ROUTE_SCALE = 1.0

        def _moe_forward(x, Wg, W1, W3, W2, Ws1, Ws3, Ws2):
            B, S, D = x.shape
            xt = x.reshape(-1, D)
            T = xt.shape[0]
            scores = jax.nn.softmax(xt @ Wg.T, axis=-1)
            sg = scores.reshape(T, G, E // G)
            group_scores = sg.max(axis=-1)
            gidx = jax.lax.top_k(group_scores, TOPK_G)[1]
            gmask = jax.nn.one_hot(gidx, G, dtype=jnp.float32).sum(axis=1) > 0
            masked = jnp.where(gmask[:, :, None], sg, -jnp.inf).reshape(T, E)
            topi = jax.lax.top_k(masked, TOPK)[1]
            weights = jnp.take_along_axis(scores, topi, axis=1) * ROUTE_SCALE
            combine = jnp.zeros((T, E), xt.dtype).at[jnp.arange(T)[:, None], topi].add(weights)
            h = jax.nn.silu(jnp.einsum('td,eid->eti', xt, W1)) * jnp.einsum('td,eid->eti', xt, W3)
            expert_out = jnp.einsum('eti,edi->etd', h, W2)
            y = jnp.einsum('etd,te->td', expert_out, combine)
            z = jax.nn.silu(xt @ Ws1.T) * (xt @ Ws3.T) @ Ws2.T
            return (y + z).reshape(B, S, D)
        return _moe_forward(x, Wg, W1, W3, W2, Ws1, Ws3, Ws2)
    x = x + _L0_xattn_ref(16, 128, 256, L0_xattn_time_decay, L0_xattn_time_first, _layernorm(x, axis=-1), ctx_2048)
    x = x + _L0_ffn_ref(_layernorm(x, axis=-1), L0_ffn_Wg, L0_ffn_W1, L0_ffn_W3, L0_ffn_W2, L0_ffn_Ws1, L0_ffn_Ws3, L0_ffn_Ws2)
    return x

_drawn_inputs = setup_inputs


def setup_inputs(seed=0):
    import zlib

    import numpy as np

    out = dict(_drawn_inputs(seed))
    spreads = {}
    factors = {'L0_ffn_Wg': 8.0,
     'L0_ffn_W1': 8.0,
     'L0_ffn_W3': 8.0,
     'L0_ffn_W2': 8.0,
     'L0_ffn_Ws1': 3.623,
     'L0_ffn_Ws3': 3.579,
     'L0_ffn_Ws2': 3.575}
    for name, (base, spread) in spreads.items():
        noise = np.random.default_rng([zlib.crc32(name.encode()), seed]).standard_normal(out[name].shape)
        drawn = base * np.exp(spread * noise) if base else spread * noise
        out[name] = jnp.asarray(drawn.astype(out[name].dtype))
    for name, factor in factors.items():
        out[name] = (out[name] * factor).astype(out[name].dtype)
    return out
```

```python
from contextlib import ExitStack

import numpy as np

import concourse.bass as bass
from concourse import mybir

ALU = mybir.AluOpType
ACT = mybir.ActivationFunctionType
AX = mybir.AxisListType
F32 = mybir.dt.float32
F32R = mybir.dt.float32r
BF16 = mybir.dt.bfloat16
F16 = mybir.dt.float16
I32 = mybir.dt.int32
U32 = mybir.dt.uint32

P = 128
NB = 16
C = 256
NT = NB * P
E = 16
NS = 2
NG, GS = 4, 4
TOP, TOP_G = 4, 2
I = 176
IH = I // 2
GB = 4
G = NB // GB
N = GB * P
BLK = NT * TOP // P + E - 1
BW = BLK + 1
LATE = 8
LAST = 3
NEG = -1e38
EPS = 1e-5
PAD = 100000.0


def ds(start, size):
    return bass.ds(start, size)


def xattn_moe_kernel(nc, x, ctx, decay, first, wg, w13, w2, out):
    xhat_dram = nc.dram_tensor("xhat_rows", [NT, C], F32, kind="Internal").ap()
    pair_dram = nc.dram_tensor("pair_rows", [TOP * NT, C], F32, kind="Internal").ap()
    x_t = x.rearrange("b t c -> t b c")
    out_t = out.rearrange("b t c -> t b c")
    xhat_t = xhat_dram.rearrange("(j p) c -> p j c", p=P)
    pair_t = pair_dram.rearrange("(k j p) c -> p k j c", p=P, k=TOP)

    with ExitStack() as stack:
        top = [(nc.sbuf_base + 63) // 64 * 64]

        def place(name, shape, dt, at=None):
            size = int(np.prod(shape[1:])) * mybir.dt.size(dt)
            size = (size + 31) // 32 * 32
            where = top if at is None else at
            t = nc.alloc_sbuf_tensor_at(name, shape, dt, offset=where[0])
            where[0] += size
            return t

        SL = NS + E
        here = [top[0]]
        w13_hi = place("w13_hi", [P, SL, 2, 2 * I], F32R)
        at_lo13 = [top[0]]
        w13_lo = place("w13_lo", [P, SL, 2, 2 * I], F32R)
        at_hi2 = [top[0]]
        w2_hi = place("w2_hi", [P, SL, 2, C], F32R)
        at_lo2 = [top[0]]
        w2_lo = place("w2_lo", [P, SL, 2, C], F32R)
        w13_raw = place("w13_raw", [P, SL, 2, 2 * I], F32, [at_lo13[0]])
        w2_raw = place("w2_raw", [P, SL, 2, C], F32, [at_lo2[0]])
        early13 = (SL - LATE) * 2 * 2 * I * 4
        early2 = (SL - LATE) * 2 * C * 4
        z1, z2 = [here[0] + early13], [at_lo13[0] + early13]
        z3, z4 = [at_hi2[0] + early2], [at_lo2[0] + early2]

        base = place("base", [P, NB, C], F32)
        x_hi = place("x_hi", [P, 2, 2, P], F32R)
        x_lo = place("x_lo", [P, 2, 2, P], F32R)
        h = place("h", [P, 2, I], F32)
        h_hi = place("h_hi", [P, 2, 2, P], F32R)
        h_lo = place("h_lo", [P, 2, 2, P], F32R)
        ident = place("ident", [P, P], F32)
        wg_raw = place("wg_raw", [P, 2, E], F32)
        wg_hi = place("wg_hi", [P, 2, E], F32R)
        wg_lo = place("wg_lo", [P, 2, E], F32R)
        logits = place("logits", [P, NB, E], F32)
        topv = place("topv", [P, NB, 8], F32)
        rows_in = place("rows_in", [P, BW], I32)
        rows_out = place("rows_out", [P, BW], I32)
        block_slot = place("block_slot", [1, BW], I32)
        before = place("before", [P, P], BF16)
        ones = place("ones", [P, P], BF16)
        iota_row = place("iota_row", [P, P], F32)
        token_1 = place("token_1", [P, NB], F32)
        steps = place("steps", [P, E, 16], F32)
        lower = place("lower", [P, NG, NG], F32)
        g_tail = [top[0]]
        g_rows = place("g_rows", [P, 4, C], F32)
        y_rows = place("y_rows", [P, 2, C], F32)
        assert top[0] <= nc.sbuf_usable_end, (top[0], nc.sbuf_usable_end)

        x_in = place("x_in", [P, 2, GB, C], F32, z1)
        v_in = place("v_in", [P, 2, 2, N], F32, z1)
        k_c = place("k_c", [P, 2, N], F32, z1)
        wkv_d = place("wkv_d", [P, N], F32, z1)
        clamp_pos = place("clamp_pos0", [P, 2, N], F32, z2), place("clamp_pos1", [P, 2, N], F32, z4)
        clamp_neg = place("clamp_neg0", [P, 2, N], F32, z2), place("clamp_neg1", [P, 2, N], F32, z4)
        kv = place("kv0", [P, 2, N], F32, z2), place("kv1", [P, 2, N], F32, z4)
        k_t = place("k_t", [P, GB, C], F32, z2)
        decay_row = place("decay_row", [P, 2, N], F32, z2)
        num = place("num0", [P, N], F32, z2), place("num1", [P, N], F32, z4)
        den = place("den", [P, N], F32, z3)
        pp = place("pp0", [P, N + 1], F32, z3), place("pp1", [P, N + 1], F32, z3)
        aa = place("aa", [P, N + 1], F32, z3)
        bb = place("bb", [P, N + 1], F32, z3)
        xhat = place("xhat", [P, GB, C], F32, z3)
        td = place("td", [P, 2], F32, z3)
        tf = place("tf", [P, 2], F32, z3)
        wdec = place("wdec", [P, 2], F32, z3)
        stats = place("stats", [P, GB, 6], F32, z3)
        mv = place("mv", [P, GB, 2], F32, z3), place("mv2", [P, GB, 2], F32, z3)
        vpe = place("vpe", [P, GB], F32, z3)
        rstd = place("rstd", [P, GB], F32, z3), place("rstd2", [P, GB], F32, z3)
        half_neg = place("half_neg", [P, GB], F32, z3)
        assert z1[0] <= here[0] + SL * 4 * I * 4 and z2[0] <= at_lo13[0] + SL * 4 * I * 4
        assert z3[0] <= at_hi2[0] + SL * 2 * C * 4 and z4[0] <= at_lo2[0] + SL * 2 * C * 4, z4

        r1 = [g_tail[0]]
        score = place("score", [P, NB, E], F32, r1)
        masked = place("masked", [P, NB, E], F32, r1)
        total = place("total", [P, E, NB], F32, r1)
        pos = place("pos", [P, NB, E], F32, r1)
        assert r1[0] <= top[0], (r1[0], top[0])
        last13, last2 = LAST * 4 * I * 4, LAST * 2 * C * 4
        t1 = [here[0] + SL * 4 * I * 4 - last13]
        onehot = place("onehot", [P, NB * TOP, E], F32, t1)
        cmp_gt = place("cmp_gt", [P, NB, E], F32, t1)
        t2 = [at_lo13[0] + SL * 4 * I * 4 - last13]
        picked = place("picked", [P, NB * TOP, E], F32, t2)
        cmp_eq = place("cmp_eq", [P, NB, E], F32, t2)
        RING = 16
        t3 = [at_hi2[0] + SL * 2 * C * 4 - last2]
        hot_q = place("hot_q", [P, RING, P], F16, t3)
        t4 = [at_lo2[0] + SL * 2 * C * 4 - last2]
        hot_blk = place("hot_blk", [P, RING, BW], F16, t4)
        listed = place("listed", [P, TOP, BW], F32, t1)
        grp = place("grp", [P, NB * NG], F32, t3)
        grank = place("grank", [P, NB * NG], F32, t3)
        gmask = place("gmask", [P, NB * NG], F32, t3)
        tmax = place("tmax", [P, NB], F32, t3)
        tsum = place("tsum", [P, NB], F32, t3)
        trec = place("trec", [P, NB], F32, t3)
        topi = place("topi", [P, NB, 8], U32, t4)
        nblk = place("nblk", [P, E], F32, t3)
        bend = place("bend", [P, E], F32, t3)
        bstart = place("bstart", [P, E], F32, t4)
        posk = place("posk", [P, NB * TOP], F32, t4)
        posi = place("posi", [P, NB * TOP], I32, t4)
        blki = place("blki", [P, NB * TOP], I32, t4)
        placei = place("placei", [P, NB * TOP], I32, t4)
        blkf = place("blkf", [P, NB * TOP], F32, t4)
        placef = place("placef", [P, NB * TOP], F32, t4)
        mask_bf = place("mask_bf", [P, NB * E], BF16, t4)
        tok = place("tok", [P, BW], F32, t2)
        filled = place("filled", [P, TOP, BW], F32, t1)
        kth = place("kth", [P, BW], F32, t2)
        rows_f = place("rows_f", [P, BW], F32, t2)
        empty = place("empty", [P, BW], F32, t2)
        slotf = place("slotf", [1, BW], F32, t2)
        reset = place("reset", [P, E, NB], F32, t2)
        assert t1[0] <= here[0] + SL * 4 * I * 4 and t2[0] <= at_lo13[0] + SL * 4 * I * 4
        assert t3[0] <= at_hi2[0] + SL * 2 * C * 4 and t4[0] <= at_lo2[0] + SL * 2 * C * 4, (t3, t4)
        pairs_in = place("pairs_in", [P, TOP, NB, C], F32, [here[0]])
        pk = [stack.enter_context(nc.psum_tensor(f"bank{i}", [P, 512], F32)) for i in range(8)]

        def sem(name):
            return stack.enter_context(nc.semaphore(name))

        def need(eng, s, count):
            if not isinstance(count, int) or count > 0:
                eng.wait_ge(s, count)

        x_loaded = [sem(f"x_loaded{i}") for i in range(2)]
        ctx_loaded = [sem(f"ctx_loaded{i}") for i in range(2)]
        small_loaded = sem("small_loaded")
        CHUNKS = [(0, 2), (2, 6), (6, SL - LATE), (SL - LATE, SL - LAST), (SL - LAST, SL)]
        w_loaded = [sem(f"w_loaded{i}") for i in range(len(CHUNKS))]
        xhat_stored = sem("xhat_stored")
        out_stored = sem("out_stored")
        pairs_loaded = [sem(f"pairs_loaded{i}") for i in range(NB // 2)]
        consts_ready = sem("consts_ready")
        pool_const = sem("pool_const")
        decay_exp = sem("decay_exp")
        stats_ready = sem("stats_ready")
        mv1_ready, rstd1_ready = sem("mv1_ready"), sem("rstd1_ready")
        mv2_ready, rstd2_ready = sem("mv2_ready"), sem("rstd2_ready")
        kt_ready = sem("kt_ready")
        kT_ready, k_ready = sem("kT_ready"), sem("k_ready")
        pp_ready, d_raw, d_ready = sem("pp_ready"), sem("d_raw"), sem("d_ready")
        clamp_ready, exp_ready, kv_ready = sem("clamp_ready"), sem("exp_ready"), sem("kv_ready")
        wkv_ready, yT_ready, x1_ready = sem("wkv_ready"), sem("yT_ready"), sem("x1_ready")
        xhat_ready = sem("xhat_ready")
        FF = {}
        for kind in ("s", "r"):
            for what in ("xT_ready", "xhi_ready", "xlo_ready", "h13_ready", "silu_ready", "h_ready", "hT_ready",
                         "hhi_ready", "hlo_ready", "y_ready"):
                FF[kind, what] = sem(f"{kind}_{what}")
        logits_copied, z_added = sem("logits_copied"), sem("z_added")
        wg_split = sem("wg_split")
        whi_ready, wlo_ready, wlo_last = sem("whi_ready"), sem("wlo_ready"), sem("wlo_last")
        vstep = sem("vstep")
        pstep = sem("pstep")
        shifted, scores_exp = sem("shifted"), sem("scores_exp")
        mask_ready, ranks_ready = sem("mask_ready"), sem("ranks_ready")
        hot_ready, hot_used, list_ready = sem("hot_ready"), sem("hot_used"), sem("list_ready")
        rows_ready, route_done = sem("rows_ready"), sem("route_done")
        gathered = [sem(f"gathered{i}") for i in range(4)]
        y_staged = sem("y_staged")
        scattered = [sem(f"scattered{i}") for i in range(2)]
        summed = sem("summed")

        block = stack.enter_context(nc.Block())

        HS = 2 * G
        UNITS = NB * NS

        def f32(ap):
            return ap.bitcast(F32)

        order = [("ln1", 0), ("key", 0), ("key", 1)]
        for g in range(G):
            order += [("max", 2 * g), ("max", 2 * g + 1), ("clamp", 2 * g), ("clamp", 2 * g + 1)]
            units = [("ffn", g - 1, n) for n in range(2 * GB + 2)] if g else []
            if g + 1 < G:
                order += [("ln1", g + 1)]
            order += units[:3] + [("wkv", 2 * g)] + units[3:7]
            if g + 1 < G:
                order += [("key", 2 * g + 2), ("key", 2 * g + 3)]
            order += [("wkv", 2 * g + 1)] + units[7:] + [("ln2", g)]
            order += [("split", 2 + 2 * g), ("split", 3 + 2 * g)]
        order += [("ffn", G - 1, n) for n in range(2 * GB + 2)]

        @block.sync
        def _(sp):
            def load_x(g):
                if g >= 2:
                    sp.wait_ge(x1_ready, 2 * (g - 1))
                sp.dma_start(x_in[:, g % 2], x_t[:, g * GB:(g + 1) * GB, :]).then_inc(x_loaded[g % 2], 16)

            def load_ctx(g):
                if g >= 2:
                    sp.wait_ge(kv_ready, 2 * (g - 1))
                sp.dma_start(v_in[:, g % 2], ctx[:, g]).then_inc(ctx_loaded[g % 2], 16)

            def load_weights(n):
                a, b = CHUNKS[n]
                sp.dma_start(w13_raw[:, a:b], w13[:, a:b]).then_inc(w_loaded[n], 16)
                sp.dma_start(w2_raw[0:IH, a:b], w2[:, a:b]).then_inc(w_loaded[n], 16)

            load_x(0)
            sp.dma_start(td[:], decay).then_inc(small_loaded, 16)
            sp.dma_start(tf[:], first).then_inc(small_loaded, 16)
            sp.dma_start(wg_raw[:], wg).then_inc(small_loaded, 16)
            load_ctx(0)
            load_x(1)
            load_weights(0)
            load_ctx(1)
            load_weights(1)
            load_weights(2)
            for g in range(G):
                sp.wait_ge(xhat_ready, GB * (g + 1))
                sp.dma_start(xhat_t[:, g * GB:(g + 1) * GB, :], xhat[:]).then_inc(xhat_stored, 16)
                if g + 2 < G:
                    load_x(g + 2)
                    load_ctx(g + 2)
            sp.wait_ge(xhat_stored, 16 * G)
            sp.wait_ge(FF["s", "xT_ready"], NB)
            load_weights(3)
            sp.wait_ge(route_done, 1)
            load_weights(4)
            sp.wait_ge(FF["r", "y_ready"], BLK)
            for i in range(2):
                sp.wait_ge(scattered[i], 16 * ((BLK + 1 - i) // 2))
            for n in range(NB // 2):
                for k in range(TOP):
                    sp.dma_start(pairs_in[:, k, 2 * n:2 * n + 2], pair_t[:, k, 2 * n:2 * n + 2]).then_inc(pairs_loaded[n], 16)
            for n in range(NB // 2):
                sp.wait_ge(summed, 2 * n + 2)
                sp.dma_start(out_t[:, 2 * n:2 * n + 2], base[:, 2 * n:2 * n + 2]).then_inc(out_stored, 16)
            sp.wait_ge(out_stored, 16 * (NB // 2))

        @block.gpsimd
        def _(pool):
            steps_done = [0]

            def step(ins):
                steps_done[0] += 1
                ins.then_inc(pstep, 1)
                return steps_done[0]

            step(pool.memset(ident[:], 0.0))
            step(pool.memset(before[:], 1.0))
            step(pool.memset(lower[:], 1.0))
            pool.memset(half_neg[:], -0.5).then_inc(pool_const, 1)
            pool.memset(ones[:], 1.0).then_inc(consts_ready, 1)
            pool.iota(iota_row[:], [[1, P]], base=0, channel_multiplier=0,
                      allow_small_or_imprecise_dtypes=True).then_inc(consts_ready, 1)
            pool.iota(token_1[:], [[P, NB]], base=1, channel_multiplier=1,
                      allow_small_or_imprecise_dtypes=True).then_inc(consts_ready, 1)
            pool.iota(steps[:], [[0, E], [P, 16]], base=0, channel_multiplier=0,
                      allow_small_or_imprecise_dtypes=True).then_inc(consts_ready, 1)
            pool.wait_ge(pstep, 3)
            pool.affine_select(out=ident[:], in_=ident[:], compare_op=ALU.not_equal, fill=1.0, base=0,
                               pattern=[[-1, P]], channel_multiplier=1).then_inc(consts_ready, 1)
            pool.affine_select(out=before[:], in_=before[:], compare_op=ALU.is_gt, fill=0.0, base=0,
                               pattern=[[1, P]], channel_multiplier=-1).then_inc(consts_ready, 1)
            pool.affine_select(out=lower[:], in_=lower[:], compare_op=ALU.is_gt, fill=0.0, base=0,
                               pattern=[[1, NG], [-1, NG]], channel_multiplier=0).then_inc(consts_ready, 1)
            pool.wait_ge(pool_const, 1)

            def power(l, g, ready, done):
                pool.wait_ge(ready, g + 1)
                n = step(pool.tensor_scalar(vpe[:], mv[l][:, :, 1], EPS, None, ALU.add))
                pool.wait_ge(pstep, n)
                pool.tensor_tensor(rstd[l][:], vpe[:], half_neg[:], ALU.pow).then_inc(done, 1)

            def split_lo(slot):
                pool.wait_ge(whi_ready, 2 * (slot + 1))
                pool.tensor_tensor(w13_lo[:, slot], w13_raw[:, slot], f32(w13_hi[:, slot]), ALU.subtract).then_inc(wlo_ready, 1)
                pool.tensor_tensor(w2_lo[0:IH, slot], w2_raw[0:IH, slot], f32(w2_hi[0:IH, slot]), ALU.subtract).then_inc(wlo_ready, 1)

            for what, *a in order:
                if what == "ln1":
                    power(0, a[0], mv1_ready, rstd1_ready)
                elif what == "ln2":
                    power(1, a[0], mv2_ready, rstd2_ready)
                elif what == "max":
                    s = a[0]
                    pool.wait_ge(pp_ready, s + 1)
                    need(pool, clamp_ready, s)
                    pool.tensor_tensor(wkv_d[:], pp[s % 2][:, 0:N], k_c[:, s % 2], ALU.subtract).then_inc(d_raw, 1)
                    pool.wait_ge(d_raw, s + 1)
                    pool.memset(wkv_d[:, 0:N:P], NEG).then_inc(d_ready, 1)
                    if s == 1:
                        split_lo(0)
                        split_lo(1)
                elif what == "clamp":
                    s = a[0]
                    pool.wait_ge(exp_ready, 2 * (s + 1))
                    pool.wait_ge(ctx_loaded[s // 2 % 2], 16 * (s // 4 + 1))
                    need(pool, wkv_ready, s - 1)
                    pool.tensor_tensor(kv[s % 2][:], clamp_pos[s % 2][:],
                                       v_in[:, s // 2 % 2, s % 2].unsqueeze(1).broadcast_to([P, 2, N]),
                                       ALU.mult).then_inc(kv_ready, 1)
                elif what == "split":
                    split_lo(a[0])
            for slot in range(SL - LATE, SL - LAST):
                split_lo(slot)
            pool.wait_ge(xhat_stored, 16 * G)
            pool.wait_ge(rows_ready, 1)

            def gather(i):
                need(pool, FF["r", "xT_ready"], i - 3)
                pool.indirect_dma_start(g_rows[:, i % 4, :], None, xhat_dram,
                                        bass.IndirectOffsetOnAxis(ap=rows_in[:, i:i + 1].bitcast(U32), axis=0)
                                        ).then_inc(gathered[i % 4], 16)

            AHEAD = 6
            for i in range(AHEAD):
                gather(i)
            for i in range(BLK):
                if i + AHEAD < BLK:
                    gather(i + AHEAD)
                pool.wait_ge(y_staged, i + 1)
                pool.indirect_dma_start(pair_dram, bass.IndirectOffsetOnAxis(ap=rows_out[:, i:i + 1].bitcast(U32), axis=0),
                                        y_rows[:, i % 2, :], None, bounds_check=TOP * NT - 1, oob_is_err=False
                                        ).then_inc(scattered[i % 2], 16)

        HT = pk[6], pk[2]
        YB = pk[7], pk[3]
        half_of = {}

        def half(i, u):
            if isinstance(i, int):
                return i // 2
            return half_of[u % 4](i)

        def run_blocks(eng, turn):
            LEAD = 3
            for i in range(LEAD):
                turn(i, i, (i + 1 < BLK, True, i >= 1, i >= 2))
            rounds = (BLK - 1 - LEAD) // 4
            with eng.Fori(0, rounds) as m:
                for u in range(4):
                    i = 4 * m + (LEAD + u)
                    half_of[(LEAD + u) % 4] = lambda _, m=m, u=u: 2 * m + (LEAD + u - 2) // 2
                    turn(i, LEAD + u, (True, True, True, True))
            for i in range(LEAD + 4 * rounds, BLK + 2):
                turn(i, i, (i + 1 < BLK, i < BLK, i - 1 < BLK, True))

        @block.scalar
        def _(act):
            act.wait_ge(small_loaded, 48)
            act.activation(wdec[:], td[:], ACT.Exp).then_inc(decay_exp, 1)
            act.activation(wg_hi[:], wg_raw[:], ACT.Copy).then_inc(wg_split, 1)

            def split_hi(slot):
                n = [n for n, (a, b) in enumerate(CHUNKS) if a <= slot < b][0]
                act.wait_ge(w_loaded[n], 32)
                act.activation(w13_hi[:, slot], w13_raw[:, slot], ACT.Copy).then_inc(whi_ready, 1)
                act.activation(w2_hi[0:IH, slot], w2_raw[0:IH, slot], ACT.Copy).then_inc(whi_ready, 1)

            def x_hi_part(kind, i, bank, free):
                act.wait_ge(FF[kind, "xT_ready"], i + 1)
                need(act, FF[kind, "h13_ready"], free)
                act.activation(x_hi[:, i % 2].rearrange("p c t -> p (c t)"), bank[:, 0:2 * P], ACT.Copy
                               ).then_inc(FF[kind, "xhi_ready"], 1)

            for what, *a in order:
                if what == "key":
                    s = a[0]
                    act.wait_ge(kT_ready, s + 1)
                    need(act, d_raw, s - 1)
                    act.activation(k_c[:, s % 2], pk[0][:], ACT.Copy).then_inc(k_ready, 1)
                    if s == 1:
                        split_hi(0)
                        split_hi(1)
                elif what == "clamp":
                    s = a[0]
                    act.wait_ge(clamp_ready, s + 1)
                    act.activation(clamp_pos[s % 2][:], clamp_pos[s % 2][:], ACT.Exp, scale=-1.0).then_inc(exp_ready, 1)
                    act.activation(clamp_neg[s % 2][:], clamp_neg[s % 2][:], ACT.Exp).then_inc(exp_ready, 1)
                elif what == "split":
                    split_hi(a[0])
                elif what == "ffn":
                    g, n = a
                    u = 2 * GB * g + n
                    if n == 0 or n % 2 and n < 2 * GB - 1:
                        t = GB * g + (n + 1) // 2
                        x_hi_part("s", t, pk[7], 2 * (t - 1))
                    if n < 2 * GB:
                        act.wait_ge(FF["s", "h13_ready"], u + 1)
                        need(act, FF["s", "hT_ready"], u - 1)
                        act.activation(h[:, u % 2], pk[4 + u % 2][:, 0:I], ACT.Silu).then_inc(FF["s", "silu_ready"], 1)
                    if 1 <= n <= 2 * GB:
                        act.wait_ge(FF["s", "hT_ready"], u)
                        need(act, FF["s", "y_ready"], u - 2)
                        act.activation(h_hi[0:IH, (u - 1) % 2].rearrange("p c t -> p (c t)"), pk[6][0:IH, 0:2 * P],
                                       ACT.Copy).then_inc(FF["s", "hhi_ready"], 1)
            for slot in range(SL - LATE, SL - LAST):
                split_hi(slot)
            act.wait_ge(shifted, 1)
            act.activation(score[:], masked[:], ACT.Exp).then_inc(scores_exp, 1)
            for slot in range(SL - LAST, SL):
                split_hi(slot)
            act.wait_ge(FF["s", "y_ready"], UNITS)

            def x_part(i, u):
                act.wait_ge(FF["r", "xT_ready"], i + 1)
                need(act, FF["r", "h13_ready"], i - 1)
                act.activation(x_hi[:, u % 2].rearrange("p c t -> p (c t)"), pk[u % 2][:, 0:2 * P], ACT.Copy
                               ).then_inc(FF["r", "xhi_ready"], 1)

            def silu(i, u):
                act.wait_ge(FF["r", "h13_ready"], i + 1)
                need(act, FF["r", "hT_ready"], i - 1)
                act.activation(h[:, u % 2], pk[4 + u % 2][:, 0:I], ACT.Silu).then_inc(FF["r", "silu_ready"], 1)

            def h_part(i, u):
                act.wait_ge(FF["r", "hT_ready"], i + 1)
                need(act, FF["r", "y_ready"], i - 1)
                act.activation(h_hi[0:IH, u % 2].rearrange("p c t -> p (c t)"), HT[u % 2][0:IH, 0:2 * P],
                               ACT.Copy).then_inc(FF["r", "hhi_ready"], 1)

            def stage(i, u, turn):
                act.wait_ge(FF["r", "y_ready"], i + 1)
                need(act, scattered[u % 2], 16 * turn)
                act.activation(y_rows[:, u % 2], YB[u % 2][:, 0:C], ACT.Copy).then_inc(y_staged, 1)

            def turn(i, u, has):
                if has[0]:
                    x_part(i + 1, u + 1)
                if has[1]:
                    silu(i, u)
                if has[2]:
                    h_part(i - 1, u + 1)
                if has[3]:
                    stage(i - 2, u, half(i - 2, u))

            x_part(0, 0)
            run_blocks(act, turn)

        @block.tensor
        def _(pe):
            pe.wait_ge(consts_ready, 7)

            def x_turn(kind, i, bank, rows):
                for c in range(2):
                    t = pe.transpose(bank[:, c * P:(c + 1) * P], rows[:, c * P:(c + 1) * P], ident[:])
                t.then_inc(FF[kind, "xT_ready"], 1)

            def products(out_, left_hi, left_lo, right_hi, right_lo):
                for c in range(2):
                    for n, (a, b) in enumerate(((left_hi, right_hi), (left_hi, right_lo), (left_lo, right_hi))):
                        m = pe.matmul(out_, a(c), b(c), start=(c == 0 and n == 0), stop=(c == 1 and n == 2))
                return m

            def gate_up(kind, b, bank, slot):
                products(bank[:, 0:2 * I], lambda c: x_hi[:, b, c], lambda c: x_lo[:, b, c],
                         lambda c: w13_hi[:, slot, c], lambda c: w13_lo[:, slot, c]).then_inc(FF[kind, "h13_ready"], 1)

            def h_turn(kind, b, bank):
                for c in range(2):
                    t = pe.transpose(bank[0:IH, c * P:(c + 1) * P], h[:, b, c * IH:(c + 1) * IH], ident[:])
                t.then_inc(FF[kind, "hT_ready"], 1)

            for what, *a in order:
                if what == "key":
                    s = a[0]
                    pe.wait_ge(kt_ready, GB * (s // 2 + 1))
                    need(pe, k_ready, s)
                    for b in range(GB):
                        t = pe.transpose(pk[0][:, b * P:(b + 1) * P], k_t[:, b, (s % 2) * P:(s % 2 + 1) * P], ident[:])
                    t.then_inc(kT_ready, 1)
                elif what == "wkv":
                    s = a[0]
                    pe.wait_ge(wkv_ready, s + 1)
                    need(pe, x1_ready, 2 * (s // 2))
                    for b in range(GB):
                        at = b % 2 * C + s % 2 * P
                        t = pe.transpose(pk[2 + b // 2][:, at:at + P], num[s % 2][:, b * P:(b + 1) * P], ident[:])
                    t.then_inc(yT_ready, 1)
                elif what == "ffn":
                    g, n = a
                    u = 2 * GB * g + n
                    if n == 0 or n % 2 and n < 2 * GB - 1:
                        t = GB * g + (n + 1) // 2
                        pe.wait_ge(xhat_ready, t + 1)
                        need(pe, FF["s", "xlo_ready"], t)
                        x_turn("s", t, pk[7], xhat[:, t % GB])
                    if n < 2 * GB:
                        need(pe, FF["s", "h_ready"], u - 1)
                        if n % 2 == 0:
                            t = u // 2
                            pe.wait_ge(FF["s", "xlo_ready"], t + 1)
                            pe.wait_ge(wg_split, 2)
                            need(pe, logits_copied, t)
                            for c in range(2):
                                for m, (l, r) in enumerate(((x_hi, wg_hi), (x_hi, wg_lo), (x_lo, wg_hi), (x_lo, wg_lo))):
                                    pe.matmul(pk[4][:, 2 * I:2 * I + E], l[:, t % 2, c], r[:, c],
                                              start=(c == 0 and m == 0), stop=(c == 1 and m == 3))
                            pe.wait_ge(wlo_ready, 4)
                        gate_up("s", u // 2 % 2, pk[4 + u % 2], u % 2)
                    if 1 <= n <= 2 * GB:
                        pe.wait_ge(FF["s", "h_ready"], u)
                        need(pe, FF["s", "hlo_ready"], u - 1)
                        h_turn("s", (u - 1) % 2, pk[6])
                    if n >= 2:
                        w = u - 2
                        pe.wait_ge(FF["s", "hlo_ready"], w + 1)
                        if w % 2 == 0:
                            need(pe, z_added, w // 2)
                        k = 0
                        for c in range(2):
                            for l, r in ((h_hi, w2_hi), (h_hi, w2_lo), (h_lo, w2_hi)):
                                m = pe.matmul(pk[1][:, 0:C], l[0:IH, w % 2, c], r[0:IH, w % 2, c],
                                              start=(w % 2 == 0 and k == 0), stop=(w % 2 == 1 and k == 5))
                                k += 1
                        m.then_inc(FF["s", "y_ready"], 1)
            pe.wait_ge(mask_ready, 1)
            pe.matmul(pk[0][:, 0:NB * E], before[:], mask_bf[:], start=True, stop=True).then_inc(ranks_ready, 1)
            pe.matmul(pk[2][:, 0:NB * E], ones[:], mask_bf[:], start=True, stop=True).then_inc(ranks_ready, 1)
            for k in range(TOP):
                for j in range(NB):
                    n = k * NB + j
                    pe.wait_ge(hot_ready, n + 1)
                    pe.matmul(pk[3][:, k * BW:(k + 1) * BW], hot_q[:, n % RING], hot_blk[:, n % RING],
                              start=(j == 0), stop=(j == NB - 1)).then_inc(hot_used, 1)
            pe.wait_ge(rows_ready, 1)
            pe.wait_ge(wlo_ready, 2 * (SL - LAST))
            pe.wait_ge(wlo_last, 2 * LAST)

            def x_step(i, u, turn_):
                pe.wait_ge(gathered[u % 4], 16 * turn_ + 16)
                need(pe, FF["r", "xlo_ready"], i - 1)
                x_turn("r", i, pk[u % 2], g_rows[:, u % 4])

            def quarter(i, u):
                if isinstance(i, int):
                    return i // 4
                return quarter_of[u]

            quarter_of = {}

            def slot_of(i):
                at = i if isinstance(i, int) else None
                ap = block_slot[0:1, at:at + 1] if at is not None else block_slot[0:1, ds(i, 1)]
                return pe.value_load(ap, min_val=NS, max_val=SL - 1)

            def turn(i, u, has):
                if not isinstance(i, int):
                    first = loop_m[0]
                if has[0]:
                    n = (i + 1) // 4 if isinstance(i, int) else loop_m[0] + (u + 1) // 4
                    x_step(i + 1, u + 1, n)
                if has[1]:
                    slot = slot_of(i)
                    pe.wait_ge(FF["r", "xlo_ready"], i + 1)
                    need(pe, FF["r", "h_ready"], i - 1)
                    products(pk[4 + u % 2][:, 0:2 * I], lambda c: x_hi[:, u % 2, c], lambda c: x_lo[:, u % 2, c],
                             lambda c: w13_hi[:, ds(slot, 1), c], lambda c: w13_lo[:, ds(slot, 1), c]
                             ).then_inc(FF["r", "h13_ready"], 1)
                if has[2]:
                    pe.wait_ge(FF["r", "h_ready"], i)
                    need(pe, FF["r", "hlo_ready"], i - 2)
                    h_turn("r", (u + 1) % 2, HT[(u + 1) % 2])
                if has[3]:
                    slot = slot_of(i - 2)
                    pe.wait_ge(FF["r", "hlo_ready"], i - 1)
                    need(pe, y_staged, i - 3)
                    products(YB[u % 2][:, 0:C], lambda c: h_hi[0:IH, u % 2, c], lambda c: h_lo[0:IH, u % 2, c],
                             lambda c: w2_hi[0:IH, ds(slot, 1), c], lambda c: w2_lo[0:IH, ds(slot, 1), c]
                             ).then_inc(FF["r", "y_ready"], 1)

            loop_m = [None]
            x_step(0, 0, 0)
            LEAD = 3
            for i in range(LEAD):
                turn(i, i, (i + 1 < BLK, True, i >= 1, i >= 2))
            rounds = (BLK - 1 - LEAD) // 4
            with pe.Fori(0, rounds) as m:
                loop_m[0] = m
                for u in range(4):
                    turn(4 * m + (LEAD + u), LEAD + u, (True, True, True, True))
            for i in range(LEAD + 4 * rounds, BLK + 2):
                turn(i, i, (i + 1 < BLK, i < BLK, i - 1 < BLK, True))

        @block.vector
        def _(dve):
            done = [0]

            def step(ins):
                done[0] += 1
                ins.then_inc(vstep, 1)
                return done[0]

            def after(n):
                dve.wait_ge(vstep, n)

            n = step(dve.memset(decay_row[:], 0.0))
            step(dve.memset(aa[:], 0.0))
            step(dve.memset(bb[:], 0.0))
            step(dve.memset(pp[0][:], NEG))
            step(dve.memset(pp[1][:], NEG))
            dve.wait_ge(decay_exp, 1)
            m = step(dve.tensor_scalar(wdec[:], wdec[:], -1.0, None, ALU.mult))
            dve.wait_ge(wg_split, 1)
            dve.tensor_tensor(wg_lo[:], wg_raw[:], f32(wg_hi[:]), ALU.subtract).then_inc(wg_split, 1)
            after(m)
            for hh in range(2):
                n = step(dve.tensor_scalar(decay_row[:, hh], decay_row[:, hh], wdec[:, hh:hh + 1], None, ALU.add))
            after(n)
            n = step(dve.memset(decay_row[:].rearrange("p h (b t) -> p h b t", t=P)[:, :, :, 0], NEG))
            after(n)

            def norm_stats(l, src, ready):
                for b in range(GB):
                    dve.bn_stats(stats[:, b], src(b)).then_inc(stats_ready, 1)
                counts[0] += GB
                dve.wait_ge(stats_ready, counts[0])
                for b in range(GB):
                    i = dve.bn_aggr(mv[l][:, b], stats[:, b])
                i.then_inc(ready, 1)

            counts = [0]

            def x_lo_part(kind, i, u, bank):
                dve.wait_ge(FF[kind, "xhi_ready"], i + 1)
                dve.tensor_tensor(x_lo[:, u % 2].rearrange("p c t -> p (c t)"), bank[:, 0:2 * P],
                                  f32(x_hi[:, u % 2]).rearrange("p c t -> p (c t)"), ALU.subtract
                                  ).then_inc(FF[kind, "xlo_ready"], 1)

            def h_mul(kind, i, u, bank):
                dve.wait_ge(FF[kind, "silu_ready"], i + 1)
                dve.tensor_tensor(h[:, u % 2], h[:, u % 2], bank[:, I:2 * I], ALU.mult).then_inc(FF[kind, "h_ready"], 1)

            def h_lo_part(kind, i, u, bank):
                dve.wait_ge(FF[kind, "hhi_ready"], i + 1)
                dve.tensor_tensor(h_lo[0:IH, u % 2].rearrange("p c t -> p (c t)"), bank[0:IH, 0:2 * P],
                                  f32(h_hi[0:IH, u % 2]).rearrange("p c t -> p (c t)"), ALU.subtract
                                  ).then_inc(FF[kind, "hlo_ready"], 1)

            for what, *a in order:
                if what == "ln1":
                    g = a[0]
                    dve.wait_ge(x_loaded[g % 2], 16 * (g // 2 + 1))
                    norm_stats(0, lambda b: x_in[:, g % 2, b], mv1_ready)
                    dve.wait_ge(rstd1_ready, g + 1)
                    need(dve, kT_ready, 2 * g)
                    for b in range(GB):
                        dve.tensor_scalar(k_t[:, b], x_in[:, g % 2, b], mv[0][:, b, 0:1], rstd[0][:, b:b + 1],
                                          ALU.subtract, ALU.mult).then_inc(kt_ready, 1)
                elif what == "max":
                    s = a[0]
                    dve.wait_ge(k_ready, s + 1)
                    need(dve, d_raw, s - 1)
                    dve.tensor_tensor_scan(pp[s % 2][:, 1:N + 1], decay_row[:, s % 2], k_c[:, s % 2], NEG,
                                           ALU.add, ALU.max).then_inc(pp_ready, 1)
                elif what == "clamp":
                    s = a[0]
                    dve.wait_ge(d_ready, s + 1)
                    w, u = wdec[:, s % 2:s % 2 + 1], tf[:, s % 2:s % 2 + 1]
                    dve.tensor_scalar(clamp_pos[s % 2][:, 0], wkv_d[:], w, 0.0, ALU.add, ALU.max)
                    dve.tensor_scalar(clamp_pos[s % 2][:, 1], wkv_d[:], u, 0.0, ALU.subtract, ALU.max)
                    dve.tensor_scalar(clamp_neg[s % 2][:, 0], wkv_d[:], w, 0.0, ALU.add, ALU.min)
                    dve.tensor_scalar(clamp_neg[s % 2][:, 1], wkv_d[:], u, 0.0, ALU.subtract, ALU.min
                                      ).then_inc(clamp_ready, 1)
                elif what == "wkv":
                    s = a[0]
                    pos_, neg_, kv_ = clamp_pos[s % 2], clamp_neg[s % 2], kv[s % 2]
                    dve.wait_ge(exp_ready, 2 * (s + 1))
                    b1 = step(dve.tensor_tensor_scan(bb[:, 1:N + 1], neg_[:, 0], pos_[:, 0], 0.0, ALU.mult, ALU.add))
                    dve.wait_ge(kv_ready, s + 1)
                    a1 = step(dve.tensor_tensor_scan(aa[:, 1:N + 1], neg_[:, 0], kv_[:, 0], 0.0, ALU.mult, ALU.add))
                    after(b1)
                    b2 = step(dve.tensor_tensor(den[:], neg_[:, 1], bb[:, 0:N], ALU.mult))
                    after(a1)
                    need(dve, yT_ready, s - 1)
                    a2 = step(dve.tensor_tensor(num[s % 2][:], neg_[:, 1], aa[:, 0:N], ALU.mult))
                    after(b2)
                    b3 = step(dve.tensor_tensor(den[:], den[:], pos_[:, 1], ALU.add))
                    after(a2)
                    a3 = step(dve.tensor_tensor(num[s % 2][:], num[s % 2][:], kv_[:, 1], ALU.add))
                    after(b3)
                    b4 = step(dve.reciprocal(den[:], den[:]))
                    after(b4)
                    dve.tensor_tensor(num[s % 2][:], num[s % 2][:], den[:], ALU.mult).then_inc(wkv_ready, 1)
                elif what == "ln2":
                    g = a[0]
                    dve.wait_ge(yT_ready, 2 * g + 2)
                    for q in range(2):
                        at = GB * g + 2 * q
                        dve.tensor_tensor(base[:, at:at + 2], pk[2 + q][:].rearrange("p (b c) -> p b c", b=2),
                                          x_in[:, g % 2, 2 * q:2 * q + 2], ALU.add).then_inc(x1_ready, 1)
                    dve.wait_ge(x1_ready, 2 * g + 2)
                    norm_stats(1, lambda b: base[:, GB * g + b], mv2_ready)
                    dve.wait_ge(rstd2_ready, g + 1)
                    need(dve, xhat_stored, 16 * g)
                    need(dve, FF["s", "xT_ready"], GB * g)
                    for b in range(GB):
                        dve.tensor_scalar(xhat[:, b], base[:, GB * g + b], mv[1][:, b, 0:1], rstd[1][:, b:b + 1],
                                          ALU.subtract, ALU.mult).then_inc(xhat_ready, 1)
                elif what == "ffn":
                    g, n = a
                    u = 2 * GB * g + n
                    if n == 0 or n % 2 and n < 2 * GB - 1:
                        t = GB * g + (n + 1) // 2
                        x_lo_part("s", t, t, pk[7])
                    if n < 2 * GB:
                        h_mul("s", u, u, pk[4 + u % 2])
                        if n % 2 == 0:
                            dve.tensor_copy(logits[:, u // 2], pk[4][:, 2 * I:2 * I + E]).then_inc(logits_copied, 1)
                    if 1 <= n <= 2 * GB:
                        h_lo_part("s", u - 1, u - 1, pk[6])
                    if n >= 2 and n % 2:
                        t = (u - 3) // 2
                        dve.wait_ge(FF["s", "y_ready"], 2 * t + 2)
                        dve.tensor_tensor(base[:, t], base[:, t], pk[1][:, 0:C], ALU.add).then_inc(z_added, 1)

            def bc(ap, shape):
                return ap.broadcast_to(shape)

            dve.wait_ge(logits_copied, NB)
            n = step(dve.tensor_reduce(tmax[:], logits[:], AX.X, ALU.max))
            after(n)
            dve.tensor_tensor(masked[:], logits[:], bc(tmax[:].unsqueeze(2), [P, NB, E]), ALU.subtract).then_inc(shifted, 1)
            dve.wait_ge(scores_exp, 1)
            n = step(dve.tensor_reduce(tsum[:], score[:], AX.X, ALU.add))
            after(n)
            n = step(dve.reciprocal(trec[:], tsum[:]))
            after(n)
            n = step(dve.tensor_tensor(score[:], score[:], bc(trec[:].unsqueeze(2), [P, NB, E]), ALU.mult))
            after(n)
            n = step(dve.tensor_reduce(grp[:], score[:].rearrange("p j (g e) -> p (j g) e", g=NG), AX.X, ALU.max))
            after(n)
            gv = grp[:].rearrange("p (j g) -> p j g", g=NG)
            one = bc(gv.unsqueeze(3), [P, NB, NG, NG])
            other = bc(gv.unsqueeze(2), [P, NB, NG, NG])

            def v4(t):
                return t[:].rearrange("p j (g h) -> p j g h", g=NG)
            step(dve.tensor_tensor(v4(cmp_gt), other, one, ALU.is_gt))
            n = step(dve.tensor_tensor(v4(cmp_eq), other, one, ALU.is_equal))
            after(n)
            n = step(dve.tensor_tensor(v4(cmp_eq), v4(cmp_eq), bc(lower[:].unsqueeze(1), [P, NB, NG, NG]), ALU.mult))
            after(n)
            n = step(dve.tensor_tensor(cmp_gt[:], cmp_gt[:], cmp_eq[:], ALU.add))
            after(n)
            n = step(dve.tensor_reduce(grank[:], cmp_gt[:].rearrange("p j (g h) -> p (j g) h", g=NG), AX.X, ALU.add))
            after(n)
            n = step(dve.tensor_scalar(gmask[:], grank[:], float(TOP_G), None, ALU.is_lt))
            after(n)
            gm = bc(gmask[:].unsqueeze(2), [P, NB * NG, GS])
            mk = masked[:].rearrange("p j (g e) -> p (j g) e", g=NG)
            n = step(dve.tensor_tensor(mk, score[:].rearrange("p j (g e) -> p (j g) e", g=NG), gm, ALU.mult))
            after(n)
            n = step(dve.scalar_tensor_tensor(mk, gm, -1.0, mk, ALU.add, ALU.add))
            after(n)
            for j in range(NB):
                n = step(dve.max(topv[:, j], masked[:, j]))
            for j in range(NB):
                after(n - NB + 1 + j)
                m = step(dve.max_index(topi[:, j], topv[:, j], masked[:, j]))
            after(m)
            n = step(dve.tensor_copy(posk[:].rearrange("p (j k) -> p j k", k=TOP), topi[:, :, 0:TOP]))
            after(n)
            n = step(dve.tensor_tensor(onehot[:], bc(iota_row[:, 0:E].unsqueeze(1), [P, NB * TOP, E]),
                                       bc(posk[:].unsqueeze(2), [P, NB * TOP, E]), ALU.is_equal))
            after(n)
            oh = onehot[:].rearrange("p (j k) e -> p j e k", k=TOP)
            with nc.allow_low_precision(reason="counts of 0 or 1"):
                dve.tensor_reduce(mask_bf[:].rearrange("p (j e) -> p j e", e=E), oh, AX.X, ALU.add).then_inc(mask_ready, 1)
            n = step(dve.memset(reset[:], 1.0))
            after(n)
            step(dve.memset(reset[:, :, 0], 0.0))
            dve.wait_ge(ranks_ready, 2)
            n = step(dve.tensor_copy(total[:], pk[2][:, 0:NB * E].rearrange("p (j e) -> p e j", e=E)))
            after(n)
            flat = "p e j -> p (e j)"
            n = step(dve.tensor_tensor_scan(cmp_gt[:].rearrange(flat), reset[:].rearrange(flat), total[:].rearrange(flat), 0.0,
                                            ALU.mult, ALU.add))
            after(n)
            counts_ = cmp_gt[:][:, :, NB - 1]
            n = step(dve.tensor_tensor(cmp_eq[:], bc(counts_.unsqueeze(2), [P, E, 16]), steps[:], ALU.is_gt))
            after(n)
            n = step(dve.tensor_reduce(nblk[:], cmp_eq[:], AX.X, ALU.add))
            after(n)
            n = step(dve.tensor_tensor_scan(bend[:], ones[:, 0:E], nblk[:], 0.0, ALU.mult, ALU.add))
            after(n)
            n = step(dve.tensor_tensor(bstart[:], bend[:], nblk[:], ALU.subtract))
            m = step(dve.tensor_tensor(picked[0:1, 0:BW // 2],
                                       bc(iota_row[0:1, 0:BW // 2].unsqueeze(2), [1, BW // 2, E]),
                                       bc(bend[0:1].unsqueeze(1), [1, BW // 2, E]), ALU.is_ge))
            after(m)
            m = step(dve.tensor_reduce(slotf[:, 0:BW // 2], picked[0:1, 0:BW // 2], AX.X, ALU.add))
            after(m)
            m = step(dve.tensor_tensor(picked[0:1, 0:BW // 2],
                                       bc(iota_row[0:1, BW // 2:BW].unsqueeze(2), [1, BW // 2, E]),
                                       bc(bend[0:1].unsqueeze(1), [1, BW // 2, E]), ALU.is_ge))
            after(m)
            m = step(dve.tensor_reduce(slotf[:, BW // 2:BW], picked[0:1, 0:BW // 2], AX.X, ALU.add))
            after(m)
            m = step(dve.tensor_scalar(slotf[:], slotf[:], float(E - 1), float(NS), ALU.min, ALU.add))
            after(m)
            m = step(dve.tensor_copy(block_slot[:], slotf[:]))
            m = step(dve.tensor_tensor(cmp_gt[:], cmp_gt[:], total[:], ALU.subtract))
            after(m)
            m = step(dve.tensor_tensor(pos[:], pk[0][:, 0:NB * E].rearrange("p (j e) -> p j e", e=E),
                                       cmp_gt[:].rearrange("p e j -> p j e"), ALU.add))
            after(m)
            m = step(dve.scalar_tensor_tensor(pos[:], bc(bstart[:].unsqueeze(1), [P, NB, E]), float(P), pos[:], ALU.mult, ALU.add))
            after(m)
            m = step(dve.tensor_tensor(picked[:].rearrange("p (j k) e -> p j k e", k=TOP),
                                       onehot[:].rearrange("p (j k) e -> p j k e", k=TOP),
                                       bc(pos[:].unsqueeze(2), [P, NB, TOP, E]), ALU.mult))
            after(m)
            m = step(dve.tensor_reduce(posk[:], picked[:], AX.X, ALU.add))
            after(m)
            m = step(dve.tensor_copy(posi[:], posk[:]))
            after(m)
            step(dve.tensor_scalar(blki[:], posi[:], 7, None, ALU.arith_shift_right))
            m = step(dve.tensor_scalar(placei[:], posi[:], P - 1, None, ALU.bitwise_and))
            after(m)
            step(dve.tensor_copy(blkf[:], blki[:]))
            m = step(dve.tensor_copy(placef[:], placei[:]))
            after(m)
            for k in range(TOP):
                for j in range(NB):
                    n = k * NB + j
                    at = j * TOP + k
                    need(dve, hot_used, n - RING + 1)
                    dve.tensor_scalar(hot_q[:, n % RING], iota_row[:], placef[:, at:at + 1], None, ALU.is_equal)
                    dve.tensor_scalar(hot_blk[:, n % RING], iota_row[:, 0:BW], blkf[:, at:at + 1], token_1[:, j:j + 1],
                                      ALU.is_equal, ALU.mult).then_inc(hot_ready, 1)
            dve.wait_ge(hot_used, NB * TOP)
            n = step(dve.tensor_copy(listed[:].rearrange("p k b -> p (k b)"), pk[3][:, 0:TOP * BW]))
            after(n)
            step(dve.tensor_scalar(filled[:], listed[:], 0.5, None, ALU.is_gt))
            n = step(dve.tensor_reduce(tok[:], listed[:].rearrange("p k b -> p b k"), AX.X, ALU.add))
            after(n)
            a1 = step(dve.scalar_tensor_tensor(kth[:], filled[:, 2], 2.0, filled[:, 1], ALU.mult, ALU.add))
            step(dve.tensor_scalar(empty[:], tok[:], 0.5, PAD, ALU.is_lt, ALU.mult))
            a2 = step(dve.tensor_scalar(rows_f[:], tok[:], -1.0, 0.0, ALU.add, ALU.max))
            after(a2)
            a2 = step(dve.tensor_copy(rows_in[:], rows_f[:]))
            after(a1)
            a1 = step(dve.scalar_tensor_tensor(kth[:], filled[:, 3], 3.0, kth[:], ALU.mult, ALU.add))
            after(a1)
            a1 = step(dve.scalar_tensor_tensor(kth[:], kth[:], float(NT), tok[:], ALU.mult, ALU.add))
            after(a1)
            a1 = step(dve.scalar_tensor_tensor(kth[:], kth[:], -1.0, empty[:], ALU.add, ALU.add))
            after(a1)
            a1 = step(dve.tensor_copy(rows_out[:], kth[:]))
            after(a1)
            dve.sem_inc(rows_ready, 1)
            dve.sem_inc(route_done, 1)
            for slot in range(SL - LAST, SL):
                dve.wait_ge(whi_ready, 2 * (slot + 1))
                dve.tensor_tensor(w13_lo[:, slot], w13_raw[:, slot], f32(w13_hi[:, slot]), ALU.subtract).then_inc(wlo_last, 1)
                dve.tensor_tensor(w2_lo[0:IH, slot], w2_raw[0:IH, slot], f32(w2_hi[0:IH, slot]), ALU.subtract).then_inc(wlo_last, 1)

            def turn(i, u, has):
                if has[0]:
                    x_lo_part("r", i + 1, u + 1, pk[(u + 1) % 2])
                if has[1]:
                    h_mul("r", i, u, pk[4 + u % 2])
                if has[2]:
                    h_lo_part("r", i - 1, u + 1, HT[(u + 1) % 2])

            x_lo_part("r", 0, 0, pk[0])
            run_blocks(dve, turn)
            last = {}
            for n_ in range(NB // 2):
                dve.wait_ge(pairs_loaded[n_], 16 * TOP)
                for k in range(TOP):
                    for j in (2 * n_, 2 * n_ + 1):
                        if k:
                            after(last[j])
                        i = dve.scalar_tensor_tensor(base[:, j], pairs_in[:, k, j], topv[:, j, k:k + 1], base[:, j],
                                                     ALU.mult, ALU.add)
                        if k == TOP - 1:
                            i.then_inc(summed, 1)
                        else:
                            last[j] = step(i)


_INS = ["x", "ctx", "decay", "first", "wg", "w13", "w2"]


def kernel(x, ctx_2048, L0_xattn_time_decay, L0_xattn_time_first, L0_ffn_Wg, L0_ffn_W1, L0_ffn_W3, L0_ffn_W2,
           L0_ffn_Ws1, L0_ffn_Ws3, L0_ffn_Ws2):
    import concourse.bacc as _bacc
    from concourse.bass_utils import run_bass_kernel_spmd as _run

    a = {k: np.asarray(t) for k, t in dict(x=x, ctx=ctx_2048, decay=L0_xattn_time_decay, first=L0_xattn_time_first,
                                           wg=L0_ffn_Wg, w1=L0_ffn_W1, w3=L0_ffn_W3, w2=L0_ffn_W2, s1=L0_ffn_Ws1,
                                           s3=L0_ffn_Ws3, s2=L0_ffn_Ws2).items()}
    w1 = np.concatenate([a["s1"].reshape(NS, I, C), a["w1"]])
    w3 = np.concatenate([a["s3"].reshape(NS, I, C), a["w3"]])
    w2 = np.concatenate([a["s2"].reshape(C, NS, I).transpose(1, 0, 2), a["w2"]])
    w13 = np.concatenate([w1, w3], axis=1)
    arrays = {
        "x": a["x"],
        "ctx": a["ctx"].reshape(G, GB, P, 2, P).transpose(4, 0, 3, 1, 2).reshape(P, G, 2, N),
        "decay": a["decay"].reshape(2, P).T, "first": a["first"].reshape(2, P).T,
        "wg": a["wg"].reshape(E, 2, P).transpose(2, 1, 0),
        "w13": w13.reshape(NS + E, 2 * I, 2, P).transpose(3, 0, 2, 1),
        "w2": w2.reshape(NS + E, C, 2, IH).transpose(3, 0, 2, 1),
    }
    nc = _bacc.Bacc("TRN2", target_bir_lowering=False, num_devices=1)
    data, args = {}, []
    for name in _INS:
        t = np.ascontiguousarray(arrays[name])
        data[f"in_{name}_dram"] = t
        args.append(nc.dram_tensor(f"in_{name}_dram", t.shape, mybir.dt.from_np(t.dtype), kind="ExternalInput").ap())
    o = nc.dram_tensor("out_0_dram", (NB, P, C), F32, kind="ExternalOutput").ap()
    xattn_moe_kernel(nc, *args, o)
    r = _run(nc, [data], core_ids=[0])
    return r.results[0]["out_0_dram"]
```

```python
from contextlib import ExitStack

import numpy as np

import concourse.bass as bass
from concourse import mybir

ALU = mybir.AluOpType
ACT = mybir.ActivationFunctionType
AX = mybir.AxisListType
F32 = mybir.dt.float32
F32R = mybir.dt.float32r
BF16 = mybir.dt.bfloat16
F16 = mybir.dt.float16
I32 = mybir.dt.int32
U32 = mybir.dt.uint32

P = 128
NB = 16
C = 256
NT = NB * P
E = 16
NS = 2
NG, GS = 4, 4
TOP, TOP_G = 4, 2
I = 176
IH = I // 2
GB = 4
G = NB // GB
N = GB * P
BLK = NT * TOP // P + E - 1
BW = BLK + 1
LATE = 9
LAST = 4
NEG = -1e38
EPS = 1e-5
PAD = 100000.0


def ds(start, size):
    return bass.ds(start, size)


def xattn_moe_kernel(nc, x, ctx, decay, first, wg, w13, w2, out):
    xhat_dram = nc.dram_tensor("xhat_rows", [NT, C], F32, kind="Internal").ap()
    pair_dram = nc.dram_tensor("pair_rows", [TOP * NT, C], F32, kind="Internal").ap()
    x_t = x.rearrange("b t c -> t b c")
    out_t = out.rearrange("b t c -> t b c")
    xhat_t = xhat_dram.rearrange("(j p) c -> p j c", p=P)
    pair_t = pair_dram.rearrange("(k j p) c -> p k j c", p=P, k=TOP)

    with ExitStack() as stack:
        top = [(nc.sbuf_base + 63) // 64 * 64]

        def place(name, shape, dt, at=None):
            size = int(np.prod(shape[1:])) * mybir.dt.size(dt)
            size = (size + 31) // 32 * 32
            where = top if at is None else at
            t = nc.alloc_sbuf_tensor_at(name, shape, dt, offset=where[0])
            where[0] += size
            return t

        SL = NS + E
        here = [top[0]]
        w13_hi = place("w13_hi", [P, SL, 2, 2 * I], F32R)
        at_lo13 = [top[0]]
        w13_lo = place("w13_lo", [P, SL, 2, 2 * I], F32R)
        at_hi2 = [top[0]]
        w2_hi = place("w2_hi", [P, SL, 2, C], F32R)
        at_lo2 = [top[0]]
        w2_lo = place("w2_lo", [P, SL, 2, C], F32R)
        w13_raw = place("w13_raw", [P, SL, 2, 2 * I], F32, [at_lo13[0]])
        w2_raw = place("w2_raw", [P, SL, 2, C], F32, [at_lo2[0]])
        early13 = (SL - LATE) * 2 * 2 * I * 4
        early2 = (SL - LATE) * 2 * C * 4
        z1, z2 = [here[0] + early13], [at_lo13[0] + early13]
        z3, z4 = [at_hi2[0] + early2], [at_lo2[0] + early2]

        base = place("base", [P, NB, C], F32)
        at_x = [top[0]]
        s_x_hi = place("s_x_hi", [P, GB, 2, P], F32R)
        s_x_lo = place("s_x_lo", [P, GB, 2, P], F32R)
        x_hi = place("x_hi", [P, 2, 2, P], F32R, at_x)
        x_lo = place("x_lo", [P, 2, 2, P], F32R, at_x)
        g_rows = place("g_rows", [P, 4, C], F32, at_x)
        h = place("h", [P, 4, I], F32)
        h_hi = place("h_hi", [P, 2, 2, P], F32R)
        h_lo = place("h_lo", [P, 2, 2, P], F32R)
        ident = place("ident", [P, P], F32)
        wg_hi = place("wg_hi", [P, 2, E], F32R)
        wg_lo = place("wg_lo", [P, 2, E], F32R)
        logits = place("logits", [P, NB, E], F32)
        topv = place("topv", [P, NB, 8], F32)
        rows_in = place("rows_in", [P, BW], I32)
        rows_out = place("rows_out", [P, BW], I32)
        block_slot = place("block_slot", [1, BW], I32)
        before = place("before", [P, P], BF16)
        ones = place("ones", [P, P], BF16)
        iota_row = place("iota_row", [P, P], F16)
        steps = place("steps", [P, NB], F16)
        token_1 = place("token_1", [P, NB], F32)
        lower = place("lower", [P, NG, NG], F32)
        y_rows = place("y_rows", [P, 2, C], F32)
        assert top[0] <= nc.sbuf_usable_end, (top[0], nc.sbuf_usable_end)

        x_in = place("x_in", [P, 3, GB, C], F32, z1)
        v_in = place("v_in", [P, 2, 2, N], F32, z1)
        wkv_d = place("wkv_d", [P, N], F32, z1)
        k_c = place("k_c0", [P, N], F32, z1), place("k_c1", [P, N], F32, z2)
        clamp_pos = place("clamp_pos0", [P, 2, N], F32, z2), place("clamp_pos1", [P, 2, N], F32, z4)
        clamp_neg = place("clamp_neg0", [P, 2, N], F32, z2), place("clamp_neg1", [P, 2, N], F32, z4)
        kv = place("kv0", [P, 2, N], F32, z2), place("kv1", [P, 2, N], F32, z4)
        k_t = place("k_t", [P, GB, C], F32, z2)
        decay_row = place("decay_row", [P, 2, N], F32, z2)
        num = place("num0", [P, N], F32, z2), place("num1", [P, N], F32, z4)
        xhat = place("xhat", [P, GB, C], F32, z3)
        den = place("den", [P, N], F32, z3)
        pp = place("pp0", [P, N + 1], F32, z3), place("pp1", [P, N + 1], F32, z3)
        aa = place("aa", [P, N + 1], F32, z3)
        bb = place("bb", [P, N + 1], F32, z3)
        wg_raw = place("wg_raw", [P, 2, E], F32, z3)
        td = place("td", [P, 2], F32, z3)
        tf = place("tf", [P, 2], F32, z3)
        wdec = place("wdec", [P, 2], F32, z3)
        stats = place("stats", [P, GB, 6], F32, z3)
        mv = place("mv", [P, GB, 2], F32, z3), place("mv2", [P, GB, 2], F32, z3)
        vpe = place("vpe", [P, GB], F32, z3)
        rstd = place("rstd", [P, GB], F32, z3), place("rstd2", [P, GB], F32, z3)
        shift = place("shift", [P, GB], F32, z3), place("shift2", [P, GB], F32, z3)
        half_neg = place("half_neg", [P, GB], F32, z3)
        assert z1[0] <= here[0] + SL * 4 * I * 4 and z2[0] <= at_lo13[0] + SL * 4 * I * 4
        assert z3[0] <= at_hi2[0] + SL * 2 * C * 4 and z4[0] <= at_lo2[0] + SL * 2 * C * 4, z4

        last13, last2 = LAST * 4 * I * 4, LAST * 2 * C * 4
        t1 = [here[0] + SL * 4 * I * 4 - last13]
        onehot = place("onehot", [P, NB * TOP, E], F32, t1)
        cmp_gt = place("cmp_gt", [P, NB, E], F32, t1)
        score = place("score", [P, NB, E], F32, t1)
        masked = place("masked", [P, NB, E], F32, t1)
        t2 = [at_lo13[0] + SL * 4 * I * 4 - last13]
        picked = place("picked", [P, NB * TOP, E], F32, t2)
        cmp_eq = place("cmp_eq", [P, NB, E], F32, t2)
        total = place("total", [P, E, NB], F32, t2)
        pos = place("pos", [P, NB, E], F32, t2)
        RING = 16
        t3 = [at_hi2[0] + SL * 2 * C * 4 - last2]
        hot_q = place("hot_q", [P, RING, P], F16, t3)
        t4 = [at_lo2[0] + SL * 2 * C * 4 - last2]
        hot_blk = place("hot_blk", [P, RING, BW], F16, t4)
        listed = place("listed", [P, TOP, BW], F32, t1)
        grp = place("grp", [P, NB * NG], F32, t3)
        grank = place("grank", [P, NB * NG], F32, t3)
        gmask = place("gmask", [P, NB * NG], F32, t3)
        tmax = place("tmax", [P, NB], F32, t3)
        tsum = place("tsum", [P, NB], F32, t3)
        trec = place("trec", [P, NB], F32, t3)
        topi = place("topi", [P, NB, 8], U32, t4)
        nblk = place("nblk", [P, E], F32, t3)
        bend = place("bend", [P, E], F32, t3)
        bstart = place("bstart", [P, E], F32, t4)
        posk = place("posk", [P, NB * TOP], F32, t4)
        posi = place("posi", [P, NB * TOP], I32, t4)
        blki = place("blki", [P, NB * TOP], I32, t4)
        placei = place("placei", [P, NB * TOP], I32, t4)
        blkf = place("blkf", [P, NB * TOP], F32, t4)
        placef = place("placef", [P, NB * TOP], F32, t4)
        mask_bf = place("mask_bf", [P, NB * E], BF16, t4)
        tok = place("tok", [P, BW], F32, t2)
        filled = place("filled", [P, TOP, BW], F32, t1)
        kth = place("kth", [P, BW], F32, t2)
        rows_f = place("rows_f", [P, BW], F32, t2)
        empty = place("empty", [P, BW], F32, t2)
        slotf = place("slotf", [1, BW], F32, t2)
        reset = place("reset", [P, E, NB], F32, t2)
        assert t1[0] <= here[0] + SL * 4 * I * 4 and t2[0] <= at_lo13[0] + SL * 4 * I * 4
        assert t3[0] <= at_hi2[0] + SL * 2 * C * 4 and t4[0] <= at_lo2[0] + SL * 2 * C * 4, (t3, t4)
        pairs_in = place("pairs_in", [P, TOP, NB, C], F32, [here[0]])
        pk = [stack.enter_context(nc.psum_tensor(f"bank{i}", [P, 512], F32)) for i in range(8)]

        def sem(name):
            return stack.enter_context(nc.semaphore(name))

        def need(eng, s, count):
            if not isinstance(count, int) or count > 0:
                eng.wait_ge(s, count)

        x_loaded = [sem(f"x_loaded{i}") for i in range(3)]
        ctx_loaded = [sem(f"ctx_loaded{i}") for i in range(2)]
        small_loaded = sem("small_loaded")
        CHUNKS = [(0, 2), (2, 5), (5, SL - LATE), (SL - LATE, SL - LAST), (SL - LAST, SL)]
        w_loaded = [sem(f"w_loaded{i}") for i in range(len(CHUNKS))]
        xhat_stored = sem("xhat_stored")
        out_stored = sem("out_stored")
        pairs_loaded = [sem(f"pairs_loaded{i}") for i in range(NB // 2)]
        consts_ready = sem("consts_ready")
        pool_const = sem("pool_const")
        decay_exp = sem("decay_exp")
        stats_ready = sem("stats_ready")
        mv1_ready, rstd1_ready = sem("mv1_ready"), sem("rstd1_ready")
        mv2_ready, rstd2_ready = sem("mv2_ready"), sem("rstd2_ready")
        kt_ready = sem("kt_ready")
        kT_ready, k_ready = sem("kT_ready"), sem("k_ready")
        pp_ready, d_raw, d_ready = sem("pp_ready"), sem("d_raw"), sem("d_ready")
        clamp_ready, exp_ready, kv_ready = sem("clamp_ready"), sem("exp_ready"), sem("kv_ready")
        wkv_ready, yT_ready, x1_ready = sem("wkv_ready"), sem("yT_ready"), sem("x1_ready")
        xhat_ready = sem("xhat_ready")
        FF = {}
        for kind in ("s", "r"):
            for what in ("xT_ready", "xhi_ready", "xlo_ready", "h13_ready", "silu_ready", "h_ready", "hT_ready",
                         "hhi_ready", "hlo_ready", "y_ready"):
                FF[kind, what] = sem(f"{kind}_{what}")
        logits_ready, logits_copied, z_added, gated = sem("logits_ready"), sem("logits_copied"), sem("z_added"), sem("gated")
        wg_split = sem("wg_split")
        whi_ready, wlo_ready, wlo_last = sem("whi_ready"), sem("wlo_ready"), sem("wlo_last")
        vstep = sem("vstep")
        pstep = sem("pstep")
        shifted, scores_exp = sem("shifted"), sem("scores_exp")
        mask_ready, ranks_ready = sem("mask_ready"), sem("ranks_ready")
        hot_ready, hot_used, list_ready = sem("hot_ready"), sem("hot_used"), sem("list_ready")
        rows_ready, route_done = sem("rows_ready"), sem("route_done")
        gathered = [sem(f"gathered{i}") for i in range(4)]
        y_staged = sem("y_staged")
        scattered = [sem(f"scattered{i}") for i in range(2)]
        summed = sem("summed")

        block = stack.enter_context(nc.Block())

        HS = 2 * G
        UNITS = NB * NS

        def f32(ap):
            return ap.bitcast(F32)

        def first_part():
            done, allowed = [0], [0]

            def units(count):
                for _ in range(count):
                    if done[0] < allowed[0]:
                        yield "ffn", done[0]
                        done[0] += 1

            yield from [("ln1", 0), ("key", 0), ("key", 1), ("max", 0), ("max", 1), ("ln1", 1)]
            yield from [("split", 0), ("clamp", 0), ("clamp", 1), ("split", 1)]
            for s in range(HS):
                g, ahead = s // 2, s + 2 < HS
                if ahead:
                    yield "key", s + 2
                yield "sums", s
                yield from units(1)
                if ahead:
                    yield "max", s + 2
                yield "ratio", s
                yield from units(1)
                if ahead:
                    yield "clamp", s + 2
                yield "recip", s
                yield from units(1)
                yield "wkv", s
                if s % 2 and g + 2 < G:
                    yield "ln1", g + 2
                yield from units(1)
                yield "x1", s
                if s + 2 < SL - LATE:
                    yield "split", s + 2
                if s % 2:
                    yield from units(1)
                    yield "ln2", g
                    yield from units(UNITS)
                    for b in range(GB + 1):
                        yield "router", g, b
                    allowed[0] = 2 * GB * (g + 1)
            allowed[0] = UNITS + 4
            for part in ("scores", "top", "mask", "ranks", "blocks", "places"):
                yield part,
                yield from units(1)
            for k in range(TOP):
                yield "lists", k
                yield from units(1)
            yield from units(UNITS)

        order = list(first_part())

        @block.sync
        def _(sp):
            def load_x(g):
                if g >= 3:
                    sp.wait_ge(x1_ready, 2 * (g - 2))
                sp.dma_start(x_in[:, g % 3], x_t[:, g * GB:(g + 1) * GB, :]).then_inc(x_loaded[g % 3], 16)

            def load_ctx(g):
                if g >= 2:
                    sp.wait_ge(kv_ready, 2 * (g - 1))
                sp.dma_start(v_in[:, g % 2], ctx[:, g]).then_inc(ctx_loaded[g % 2], 16)

            def load_weights(n):
                a, b = CHUNKS[n]
                sp.dma_start(w13_raw[:, a:b], w13[:, a:b]).then_inc(w_loaded[n], 16)
                sp.dma_start(w2_raw[0:IH, a:b], w2[:, a:b]).then_inc(w_loaded[n], 16)

            load_x(0)
            sp.dma_start(td[:], decay).then_inc(small_loaded, 16)
            sp.dma_start(tf[:], first).then_inc(small_loaded, 16)
            sp.dma_start(wg_raw[:], wg).then_inc(small_loaded, 16)
            load_ctx(0)
            load_x(1)
            load_weights(0)
            load_ctx(1)
            load_x(2)
            load_weights(1)
            load_weights(2)
            load_ctx(2)
            load_x(3)
            for g in range(G):
                sp.wait_ge(xhat_ready, GB * (g + 1))
                sp.dma_start(xhat_t[:, g * GB:(g + 1) * GB, :], xhat[:]).then_inc(xhat_stored, 16)
                if g == 0:
                    load_ctx(3)
            sp.wait_ge(xhat_stored, 16 * G)
            sp.wait_ge(FF["s", "xT_ready"], NB)
            load_weights(3)
            sp.wait_ge(route_done, 1)
            load_weights(4)
            sp.wait_ge(FF["r", "y_ready"], BLK)
            for i in range(2):
                sp.wait_ge(scattered[i], 16 * ((BLK + 1 - i) // 2))
            for n in range(NB // 2):
                for k in range(TOP):
                    sp.dma_start(pairs_in[:, k, 2 * n:2 * n + 2], pair_t[:, k, 2 * n:2 * n + 2]).then_inc(pairs_loaded[n], 16)
            for n in range(NB // 2):
                sp.wait_ge(summed, 2 * n + 2)
                sp.dma_start(out_t[:, 2 * n:2 * n + 2], base[:, 2 * n:2 * n + 2]).then_inc(out_stored, 16)
            sp.wait_ge(out_stored, 16 * (NB // 2))

        @block.gpsimd
        def _(pool):
            steps_done = [0]

            def step(ins):
                steps_done[0] += 1
                ins.then_inc(pstep, 1)
                return steps_done[0]

            step(pool.memset(ident[:], 0.0))
            step(pool.memset(before[:], 1.0))
            step(pool.memset(lower[:], 1.0))
            pool.memset(half_neg[:], -0.5).then_inc(pool_const, 1)
            pool.memset(ones[:], 1.0).then_inc(consts_ready, 1)
            pool.iota(iota_row[:], [[1, P]], base=0, channel_multiplier=0,
                      allow_small_or_imprecise_dtypes=True).then_inc(consts_ready, 1)
            pool.iota(token_1[:], [[P, NB]], base=1, channel_multiplier=1,
                      allow_small_or_imprecise_dtypes=True).then_inc(consts_ready, 1)
            pool.iota(steps[:], [[P, NB]], base=0, channel_multiplier=0,
                      allow_small_or_imprecise_dtypes=True).then_inc(consts_ready, 1)
            pool.wait_ge(pstep, 3)
            pool.affine_select(out=ident[:], in_=ident[:], compare_op=ALU.not_equal, fill=1.0, base=0,
                               pattern=[[-1, P]], channel_multiplier=1).then_inc(consts_ready, 1)
            pool.affine_select(out=before[:], in_=before[:], compare_op=ALU.is_gt, fill=0.0, base=0,
                               pattern=[[1, P]], channel_multiplier=-1).then_inc(consts_ready, 1)
            pool.affine_select(out=lower[:], in_=lower[:], compare_op=ALU.is_gt, fill=0.0, base=0,
                               pattern=[[1, NG], [-1, NG]], channel_multiplier=0).then_inc(consts_ready, 1)
            pool.wait_ge(pool_const, 1)

            def power(l, g, ready, done):
                pool.wait_ge(ready, g + 1)
                n = step(pool.tensor_scalar(vpe[:], mv[l][:, :, 1], EPS, None, ALU.add))
                pool.wait_ge(pstep, n)
                need(pool, (kt_ready, xhat_ready)[l], GB * g)
                n = step(pool.tensor_tensor(rstd[l][:], vpe[:], half_neg[:], ALU.pow))
                pool.wait_ge(pstep, n)
                n = step(pool.tensor_tensor(shift[l][:], mv[l][:, :, 0], rstd[l][:], ALU.mult))
                pool.wait_ge(pstep, n)
                pool.tensor_scalar(shift[l][:], shift[l][:], -1.0, None, ALU.mult).then_inc(done, 1)

            def split_lo(slot):
                pool.wait_ge(whi_ready, 2 * (slot + 1))
                pool.tensor_tensor(w13_lo[:, slot], w13_raw[:, slot], f32(w13_hi[:, slot]), ALU.subtract).then_inc(wlo_ready, 1)
                pool.tensor_tensor(w2_lo[0:IH, slot], w2_raw[0:IH, slot], f32(w2_hi[0:IH, slot]), ALU.subtract).then_inc(wlo_ready, 1)

            for what, *a in order:
                if what == "ln1":
                    power(0, a[0], mv1_ready, rstd1_ready)
                elif what == "ln2":
                    power(1, a[0], mv2_ready, rstd2_ready)
                elif what == "max":
                    s = a[0]
                    pool.wait_ge(pp_ready, s + 1)
                    need(pool, clamp_ready, s)
                    pool.tensor_tensor(wkv_d[:], pp[s % 2][:, 0:N], k_c[s % 2][:], ALU.subtract).then_inc(d_raw, 1)
                    pool.wait_ge(d_raw, s + 1)
                    pool.memset(wkv_d[:, 0:N:P], NEG).then_inc(d_ready, 1)
                elif what == "clamp":
                    s = a[0]
                    pool.wait_ge(exp_ready, 2 * (s + 1))
                    pool.wait_ge(ctx_loaded[s // 2 % 2], 16 * (s // 4 + 1))
                    need(pool, wkv_ready, s - 1)
                    pool.tensor_tensor(kv[s % 2][:], clamp_pos[s % 2][:],
                                       v_in[:, s // 2 % 2, s % 2].unsqueeze(1).broadcast_to([P, 2, N]),
                                       ALU.mult).then_inc(kv_ready, 1)
                elif what == "split":
                    split_lo(a[0])
            for slot in range(SL - LATE, SL - LAST):
                split_lo(slot)
            pool.wait_ge(FF["s", "h13_ready"], UNITS)
            pool.wait_ge(xhat_stored, 16 * G)
            pool.wait_ge(rows_ready, 1)

            def gather(i):
                need(pool, FF["r", "xT_ready"], i - 3)
                pool.indirect_dma_start(g_rows[:, i % 4, :], None, xhat_dram,
                                        bass.IndirectOffsetOnAxis(ap=rows_in[:, i:i + 1].bitcast(U32), axis=0)
                                        ).then_inc(gathered[i % 4], 16)

            AHEAD = 8
            for i in range(AHEAD):
                gather(i)
            for i in range(BLK):
                if i + AHEAD < BLK:
                    gather(i + AHEAD)
                pool.wait_ge(y_staged, i + 1)
                pool.indirect_dma_start(pair_dram, bass.IndirectOffsetOnAxis(ap=rows_out[:, i:i + 1].bitcast(U32), axis=0),
                                        y_rows[:, i % 2, :], None, bounds_check=TOP * NT - 1, oob_is_err=False
                                        ).then_inc(scattered[i % 2], 16)

        HT = pk[6], pk[3]
        YB = pk[7], pk[2]

        def run_blocks(eng, turn, head=None):
            LEAD, END = 7, BLK + 4
            rounds = (BLK - 2 - LEAD) // 4

            def single(i):
                if head:
                    head(None, i)
                turn(i, i % 4, lambda d: 0 <= i - d < BLK, None)

            for i in range(-2, LEAD):
                single(i)
            with eng.Fori(0, rounds) as m:
                if head:
                    head(m, 4 * m + LEAD)
                for u in range(LEAD, LEAD + 4):
                    turn(4 * m + u, u, lambda d: True, m)
            for i in range(LEAD + 4 * rounds, END):
                single(i)

        @block.scalar
        def _(act):
            act.wait_ge(small_loaded, 48)
            act.activation(wdec[:], td[:], ACT.Exp).then_inc(decay_exp, 1)
            act.activation(wg_hi[:], wg_raw[:], ACT.Copy).then_inc(wg_split, 1)

            def split_hi(slot):
                n = [n for n, (a, b) in enumerate(CHUNKS) if a <= slot < b][0]
                act.wait_ge(w_loaded[n], 32)
                act.activation(w13_hi[:, slot], w13_raw[:, slot], ACT.Copy).then_inc(whi_ready, 1)
                act.activation(w2_hi[0:IH, slot], w2_raw[0:IH, slot], ACT.Copy).then_inc(whi_ready, 1)

            def x_hi_part(kind, i, bank, free):
                act.wait_ge(FF[kind, "xT_ready"], i + 1)
                need(act, FF[kind, "h13_ready"], free)
                act.activation(x_hi[:, i % 2].rearrange("p c t -> p (c t)"), bank[:, 0:2 * P], ACT.Copy
                               ).then_inc(FF[kind, "xhi_ready"], 1)

            def scale_rows(l, b, dst, src, done):
                act.activation(dst, src, ACT.Identity, bias=shift[l][:, b:b + 1], scale=rstd[l][:, b:b + 1]
                               ).then_inc(done, 1)

            for what, *a in order:
                s = a[0] if a else None
                if what == "ln1":
                    act.wait_ge(rstd1_ready, s + 1)
                    need(act, kT_ready, 2 * s)
                    for b in range(GB):
                        scale_rows(0, b, k_t[:, b], x_in[:, s % 3, b], kt_ready)
                elif what == "ln2":
                    act.wait_ge(rstd2_ready, s + 1)
                    need(act, xhat_stored, 16 * s)
                    need(act, FF["s", "xT_ready"], GB * s)
                    for b in range(GB):
                        scale_rows(1, b, xhat[:, b], base[:, GB * s + b], xhat_ready)
                elif what == "key":
                    act.wait_ge(kT_ready, s + 1)
                    need(act, d_raw, s - 1)
                    act.activation(k_c[s % 2][:], pk[0][:], ACT.Copy).then_inc(k_ready, 1)
                elif what == "clamp":
                    act.wait_ge(clamp_ready, s + 1)
                    act.activation(clamp_pos[s % 2][:], clamp_pos[s % 2][:], ACT.Exp, scale=-1.0).then_inc(exp_ready, 1)
                    act.activation(clamp_neg[s % 2][:], clamp_neg[s % 2][:], ACT.Exp).then_inc(exp_ready, 1)
                elif what == "split":
                    split_hi(s)
                elif what == "router":
                    g, b = a
                    if b < GB:
                        t = GB * g + b
                        act.wait_ge(FF["s", "xT_ready"], t + 1)
                        need(act, FF["s", "h13_ready"], 2 * (t - GB + 1))
                        act.activation(s_x_hi[:, b].rearrange("p c t -> p (c t)"), pk[7][:, 0:2 * P], ACT.Copy
                                       ).then_inc(FF["s", "xhi_ready"], 1)
                    else:
                        act.wait_ge(logits_ready, GB * (g + 1))
                        act.activation(logits[:, GB * g:GB * (g + 1)], pk[0][:, 0:GB * E].rearrange("p (b e) -> p b e", e=E),
                                       ACT.Copy).then_inc(logits_copied, GB)
                elif what == "ffn":
                    n = s
                    if n < UNITS:
                        act.wait_ge(FF["s", "h13_ready"], n + 1)
                        need(act, FF["s", "hT_ready"], n - 3)
                        act.activation(h[:, n % 4], pk[4 + n % 2][:, 0:I], ACT.Tanh, scale=0.5).then_inc(FF["s", "silu_ready"], 1)
                    w = n - 2
                    if 0 <= w < UNITS:
                        act.wait_ge(FF["s", "hT_ready"], w + 1)
                        need(act, FF["s", "y_ready"], w - 1)
                        act.activation(h_hi[0:IH, w % 2].rearrange("p c t -> p (c t)"), HT[w % 2][0:IH, 0:2 * P],
                                       ACT.Copy).then_inc(FF["s", "hhi_ready"], 1)
                elif what == "scores":
                    act.wait_ge(shifted, 1)
                    act.activation(score[:], masked[:], ACT.Exp).then_inc(scores_exp, 1)
                elif what == "blocks":
                    for slot in range(SL - LATE, SL - LAST):
                        split_hi(slot)
            for slot in range(SL - LAST, SL):
                split_hi(slot)
            act.wait_ge(FF["s", "y_ready"], UNITS)

            def x_part(i, u):
                act.wait_ge(FF["r", "xT_ready"], i + 1)
                need(act, FF["r", "h13_ready"], i - 1)
                act.activation(x_hi[:, u % 2].rearrange("p c t -> p (c t)"), pk[u % 2][:, 0:2 * P], ACT.Copy
                               ).then_inc(FF["r", "xhi_ready"], 1)

            def turn(i, u, has, m):
                if has(0):
                    act.wait_ge(FF["r", "h13_ready"], i + 1)
                    need(act, FF["r", "hT_ready"], i - 3)
                    act.activation(h[:, u % 4], pk[4 + u % 2][:, 0:I], ACT.Silu).then_inc(FF["r", "silu_ready"], 1)
                if has(-2):
                    x_part(i + 2, u + 2)
                if has(2):
                    act.wait_ge(FF["r", "hT_ready"], i - 1)
                    need(act, FF["r", "y_ready"], i - 3)
                    act.activation(h_hi[0:IH, u % 2].rearrange("p c t -> p (c t)"), HT[u % 2][0:IH, 0:2 * P],
                                   ACT.Copy).then_inc(FF["r", "hhi_ready"], 1)
                if has(4):
                    act.wait_ge(FF["r", "y_ready"], i - 3)
                    need(act, scattered[u % 2], 16 * (i // 2 - 2 if m is None else 2 * m + u // 2 - 2))
                    act.activation(y_rows[:, u % 2], YB[u % 2][:, 0:C], ACT.Copy).then_inc(y_staged, 1)

            run_blocks(act, turn)

        @block.tensor
        def _(pe):
            pe.wait_ge(consts_ready, 7)

            def x_turn(kind, i, bank, rows):
                for c in range(2):
                    t = pe.transpose(bank[:, c * P:(c + 1) * P], rows[:, c * P:(c + 1) * P], ident[:])
                t.then_inc(FF[kind, "xT_ready"], 1)

            def products(out_, left_hi, left_lo, right_hi, right_lo):
                for c in range(2):
                    for n, (a, b) in enumerate(((left_hi, right_hi), (left_hi, right_lo), (left_lo, right_hi))):
                        m = pe.matmul(out_, a(c), b(c), start=(c == 0 and n == 0), stop=(c == 1 and n == 2))
                return m

            def h_turn(kind, b, bank):
                for c in range(2):
                    t = pe.transpose(bank[0:IH, c * P:(c + 1) * P], h[:, b, c * IH:(c + 1) * IH], ident[:])
                t.then_inc(FF[kind, "hT_ready"], 1)

            for what, *a in order:
                s = a[0] if a else None
                if what == "key":
                    pe.wait_ge(kt_ready, GB * (s // 2 + 1))
                    need(pe, k_ready, s)
                    if s % 2 == 0:
                        need(pe, logits_copied, GB * (s // 2 - 1))
                    for b in range(GB):
                        t = pe.transpose(pk[0][:, b * P:(b + 1) * P], k_t[:, b, (s % 2) * P:(s % 2 + 1) * P], ident[:])
                    t.then_inc(kT_ready, 1)
                elif what == "wkv":
                    pe.wait_ge(wkv_ready, s + 1)
                    need(pe, x1_ready, s)
                    for b in range(GB):
                        t = pe.transpose(pk[2][:, b * P:(b + 1) * P], num[s % 2][:, b * P:(b + 1) * P], ident[:])
                    t.then_inc(yT_ready, 1)
                elif what == "router":
                    g, b = a
                    t = GB * g + b
                    if b < GB:
                        pe.wait_ge(xhat_ready, t + 1)
                        need(pe, FF["s", "xlo_ready"], t)
                        x_turn("s", t, pk[7], xhat[:, b])
                    if b:
                        t -= 1
                        pe.wait_ge(FF["s", "xlo_ready"], t + 1)
                        pe.wait_ge(wg_split, 2)
                        if b == 1:
                            pe.wait_ge(k_ready, min(2 * g + 4, HS))
                        for c in range(2):
                            for m, (l, r) in enumerate(((s_x_hi, wg_hi), (s_x_hi, wg_lo), (s_x_lo, wg_hi), (s_x_lo, wg_lo))):
                                m_ = pe.matmul(pk[0][:, (b - 1) * E:b * E], l[:, b - 1, c], r[:, c],
                                               start=(c == 0 and m == 0), stop=(c == 1 and m == 3))
                        m_.then_inc(logits_ready, 1)
                elif what == "ffn":
                    n = s
                    if n < UNITS:
                        if n == 0:
                            pe.wait_ge(wlo_ready, 4)
                        need(pe, FF["s", "h_ready"], n - 1)
                        b = n // 2 % GB
                        products(pk[4 + n % 2][:, 0:2 * I], lambda c: s_x_hi[:, b, c], lambda c: s_x_lo[:, b, c],
                                 lambda c: w13_hi[:, n % 2, c], lambda c: w13_lo[:, n % 2, c]
                                 ).then_inc(FF["s", "h13_ready"], 1)
                    w = n - 4
                    if w >= 0:
                        pe.wait_ge(FF["s", "hlo_ready"], w + 1)
                        if w % 2 == 0:
                            need(pe, z_added, w // 2)
                        k = 0
                        for c in range(2):
                            for l, r in ((h_hi, w2_hi), (h_hi, w2_lo), (h_lo, w2_hi)):
                                m = pe.matmul(pk[1][:, 0:C], l[0:IH, w % 2, c], r[0:IH, w % 2, c],
                                              start=(w % 2 == 0 and k == 0), stop=(w % 2 == 1 and k == 5))
                                k += 1
                        m.then_inc(FF["s", "y_ready"], 1)
                    w = n - 2
                    if 0 <= w < UNITS:
                        pe.wait_ge(FF["s", "h_ready"], w + 1)
                        need(pe, FF["s", "hlo_ready"], w - 1)
                        h_turn("s", w % 4, HT[w % 2])
                elif what == "ranks":
                    pe.wait_ge(mask_ready, 1)
                    pe.matmul(pk[0][:, 0:NB * E], before[:], mask_bf[:], start=True, stop=True)
                    pe.matmul(pk[2][:, 0:NB * E], ones[:], mask_bf[:], start=True, stop=True).then_inc(ranks_ready, 1)
                elif what == "lists":
                    for j in range(NB):
                        n = s * NB + j
                        pe.wait_ge(hot_ready, n + 1)
                        pe.matmul(pk[7][:, s * BW:(s + 1) * BW], hot_q[:, n % RING], hot_blk[:, n % RING],
                                  start=(j == 0), stop=(j == NB - 1)).then_inc(hot_used, 1)
            pe.wait_ge(z_added, NB)
            pe.wait_ge(rows_ready, 1)
            pe.wait_ge(wlo_ready, 2 * (SL - LAST))
            pe.wait_ge(wlo_last, 2 * LAST)
            slots = {}

            def head(m, i):
                count = 4 if m is not None else 1
                for stage, at in (("first", i), ("second", i - 4)):
                    if m is None and not 0 <= at < BLK:
                        continue
                    ap = block_slot[0:1, at:at + 1] if m is None else block_slot[0:1, ds(at, count)]
                    _, got = nc.values_load_multi_w_load_instructions(
                        ap, engines=(mybir.EngineType.PE,), min_val=NS, max_val=SL - 1,
                        skip_runtime_bounds_check_because="clamped when computed")
                    slots[stage] = got

            def turn(i, u, has, m):
                n = 0 if m is None else u - 7
                if has(-2):
                    pe.wait_ge(gathered[(u + 2) % 4], 16 * ((i + 2) // 4 + 1 if m is None else m + (u + 2) // 4 + 1))
                    need(pe, FF["r", "xlo_ready"], i + 1)
                    x_turn("r", i, pk[u % 2], g_rows[:, (u + 2) % 4])
                if has(0):
                    slot = slots["first"][n]
                    pe.wait_ge(FF["r", "xlo_ready"], i + 1)
                    need(pe, FF["r", "h_ready"], i - 1)
                    products(pk[4 + u % 2][:, 0:2 * I], lambda c: x_hi[:, u % 2, c], lambda c: x_lo[:, u % 2, c],
                             lambda c: w13_hi[:, ds(slot, 1), c], lambda c: w13_lo[:, ds(slot, 1), c]
                             ).then_inc(FF["r", "h13_ready"], 1)
                if has(4):
                    slot = slots["second"][n]
                    pe.wait_ge(FF["r", "hlo_ready"], i - 3)
                    need(pe, y_staged, i - 5)
                    products(YB[u % 2][:, 0:C], lambda c: h_hi[0:IH, u % 2, c], lambda c: h_lo[0:IH, u % 2, c],
                             lambda c: w2_hi[0:IH, ds(slot, 1), c], lambda c: w2_lo[0:IH, ds(slot, 1), c]
                             ).then_inc(FF["r", "y_ready"], 1)
                if has(2):
                    pe.wait_ge(FF["r", "h_ready"], i - 1)
                    need(pe, FF["r", "hlo_ready"], i - 3)
                    h_turn("r", (u + 2) % 4, HT[u % 2])

            run_blocks(pe, turn, head)

        @block.vector
        def _(dve):
            done = [0]

            def step(ins):
                done[0] += 1
                ins.then_inc(vstep, 1)
                return done[0]

            def after(n):
                dve.wait_ge(vstep, n)

            n = step(dve.memset(decay_row[:], 0.0))
            step(dve.memset(aa[:], 0.0))
            step(dve.memset(bb[:], 0.0))
            step(dve.memset(pp[0][:], NEG))
            step(dve.memset(pp[1][:], NEG))
            dve.wait_ge(decay_exp, 1)
            m = step(dve.tensor_scalar(wdec[:], wdec[:], -1.0, None, ALU.mult))
            dve.wait_ge(wg_split, 1)
            dve.tensor_tensor(wg_lo[:], wg_raw[:], f32(wg_hi[:]), ALU.subtract).then_inc(wg_split, 1)
            after(m)
            for hh in range(2):
                n = step(dve.tensor_scalar(decay_row[:, hh], decay_row[:, hh], wdec[:, hh:hh + 1], None, ALU.add))
            after(n)
            n = step(dve.memset(decay_row[:].rearrange("p h (b t) -> p h b t", t=P)[:, :, :, 0], NEG))
            after(n)

            def norm_stats(l, src, ready):
                for b in range(GB):
                    dve.bn_stats(stats[:, b], src(b)).then_inc(stats_ready, 1)
                counts[0] += GB
                dve.wait_ge(stats_ready, counts[0])
                for b in range(GB):
                    i = dve.bn_aggr(mv[l][:, b], stats[:, b])
                i.then_inc(ready, 1)

            counts = [0]

            def x_lo_part(kind, i, lo, hi, bank):
                dve.wait_ge(FF[kind, "xhi_ready"], i + 1)
                dve.tensor_tensor(lo.rearrange("p c t -> p (c t)"), bank[:, 0:2 * P],
                                  f32(hi).rearrange("p c t -> p (c t)"), ALU.subtract
                                  ).then_inc(FF[kind, "xlo_ready"], 1)

            def h_lo_part(kind, i, u, bank):
                dve.wait_ge(FF[kind, "hhi_ready"], i + 1)
                dve.tensor_tensor(h_lo[0:IH, u % 2].rearrange("p c t -> p (c t)"), bank[0:IH, 0:2 * P],
                                  f32(h_hi[0:IH, u % 2]).rearrange("p c t -> p (c t)"), ALU.subtract
                                  ).then_inc(FF[kind, "hlo_ready"], 1)

            mark = {}

            def ffn(n):
                u = n - 1
                if 0 <= u < UNITS:
                    dve.wait_ge(FF["s", "silu_ready"], u + 1)
                    bank = pk[4 + u % 2]
                    dve.scalar_tensor_tensor(h[:, u % 4], h[:, u % 4], 1.0, bank[:, 0:I], ALU.add, ALU.mult).then_inc(gated, 1)
                    dve.wait_ge(gated, u + 1)
                    dve.tensor_tensor(h[:, u % 4], h[:, u % 4], bank[:, I:2 * I], ALU.mult).then_inc(FF["s", "h_ready"], 1)
                w = n - 3
                if 0 <= w < UNITS:
                    h_lo_part("s", w, w, HT[w % 2])
                if n >= 6 and n % 2 == 0:
                    add_z((n - 6) // 2)

            def add_z(t):
                dve.wait_ge(FF["s", "y_ready"], 2 * t + 2)
                dve.scalar_tensor_tensor(base[:, t], pk[1][:, 0:C], 0.5, base[:, t], ALU.mult, ALU.add).then_inc(z_added, 1)

            def recurrence(what, s):
                g = s // 2
                if what == "max":
                    dve.wait_ge(k_ready, s + 1)
                    need(dve, d_raw, s - 1)
                    dve.tensor_tensor_scan(pp[s % 2][:, 1:N + 1], decay_row[:, s % 2], k_c[s % 2][:], NEG,
                                           ALU.add, ALU.max).then_inc(pp_ready, 1)
                elif what == "clamp":
                    dve.wait_ge(d_ready, s + 1)
                    if s >= 2:
                        after(mark["a"])
                    w, u = wdec[:, s % 2:s % 2 + 1], tf[:, s % 2:s % 2 + 1]
                    dve.tensor_scalar(clamp_pos[s % 2][:, 0], wkv_d[:], w, 0.0, ALU.add, ALU.max)
                    dve.tensor_scalar(clamp_pos[s % 2][:, 1], wkv_d[:], u, 0.0, ALU.subtract, ALU.max)
                    dve.tensor_scalar(clamp_neg[s % 2][:, 0], wkv_d[:], w, 0.0, ALU.add, ALU.min)
                    dve.tensor_scalar(clamp_neg[s % 2][:, 1], wkv_d[:], u, 0.0, ALU.subtract, ALU.min
                                      ).then_inc(clamp_ready, 1)
                pos_, neg_, kv_ = clamp_pos[s % 2], clamp_neg[s % 2], kv[s % 2]
                if what == "sums":
                    dve.wait_ge(exp_ready, 2 * (s + 1))
                    mark["b"] = step(dve.tensor_tensor_scan(bb[:, 1:N + 1], neg_[:, 0], pos_[:, 0], 0.0, ALU.mult, ALU.add))
                    dve.wait_ge(kv_ready, s + 1)
                    mark["a"] = step(dve.tensor_tensor_scan(aa[:, 1:N + 1], neg_[:, 0], kv_[:, 0], 0.0, ALU.mult, ALU.add))
                elif what == "ratio":
                    after(mark["b"])
                    b2 = step(dve.tensor_tensor(den[:], neg_[:, 1], bb[:, 0:N], ALU.mult))
                    after(mark["a"])
                    need(dve, yT_ready, s - 1)
                    a2 = step(dve.tensor_tensor(num[s % 2][:], neg_[:, 1], aa[:, 0:N], ALU.mult))
                    after(b2)
                    mark["b"] = step(dve.tensor_tensor(den[:], den[:], pos_[:, 1], ALU.add))
                    after(a2)
                    mark["a"] = step(dve.tensor_tensor(num[s % 2][:], num[s % 2][:], kv_[:, 1], ALU.add))
                elif what == "recip":
                    after(mark["b"])
                    mark["b"] = step(dve.reciprocal(den[:], den[:]))
                elif what == "wkv":
                    after(mark["b"])
                    dve.tensor_tensor(num[s % 2][:], num[s % 2][:], den[:], ALU.mult).then_inc(wkv_ready, 1)
                elif what == "x1":
                    dve.wait_ge(yT_ready, s + 1)
                    cols = slice(s % 2 * P, (s % 2 + 1) * P)
                    dve.tensor_tensor(base[:, GB * g:GB * (g + 1), cols], pk[2][:].rearrange("p (b c) -> p b c", b=GB),
                                      x_in[:, g % 3, :, cols], ALU.add).then_inc(x1_ready, 1)

            def norms(what, g):
                if what == "ln1":
                    dve.wait_ge(x_loaded[g % 3], 16 * (g // 3 + 1))
                    need(dve, rstd1_ready, g)
                    norm_stats(0, lambda b: x_in[:, g % 3, b], mv1_ready)
                else:
                    dve.wait_ge(x1_ready, 2 * g + 2)
                    need(dve, rstd2_ready, g)
                    norm_stats(1, lambda b: base[:, GB * g + b], mv2_ready)

            def bc(ap, shape):
                return ap.broadcast_to(shape)

            def scores():
                dve.wait_ge(logits_copied, NB)
                n = step(dve.tensor_reduce(tmax[:], logits[:], AX.X, ALU.max))
                after(n)
                dve.tensor_tensor(masked[:], logits[:], bc(tmax[:].unsqueeze(2), [P, NB, E]), ALU.subtract).then_inc(shifted, 1)
                dve.wait_ge(scores_exp, 1)
                n = step(dve.tensor_reduce(tsum[:], score[:], AX.X, ALU.add))
                after(n)
                n = step(dve.reciprocal(trec[:], tsum[:]))
                after(n)
                n = step(dve.tensor_tensor(score[:], score[:], bc(trec[:].unsqueeze(2), [P, NB, E]), ALU.mult))
                after(n)
                n = step(dve.tensor_reduce(grp[:], score[:].rearrange("p j (g e) -> p (j g) e", g=NG), AX.X, ALU.max))
                after(n)
                gv = grp[:].rearrange("p (j g) -> p j g", g=NG)
                one = bc(gv.unsqueeze(3), [P, NB, NG, NG])
                other = bc(gv.unsqueeze(2), [P, NB, NG, NG])

                def v4(t):
                    return t[:].rearrange("p j (g h) -> p j g h", g=NG)
                step(dve.tensor_tensor(v4(cmp_gt), other, one, ALU.is_gt))
                n = step(dve.tensor_tensor(v4(cmp_eq), other, one, ALU.is_equal))
                after(n)
                n = step(dve.tensor_tensor(v4(cmp_eq), v4(cmp_eq), bc(lower[:].unsqueeze(1), [P, NB, NG, NG]), ALU.mult))
                after(n)
                n = step(dve.tensor_tensor(cmp_gt[:], cmp_gt[:], cmp_eq[:], ALU.add))
                after(n)
                n = step(dve.tensor_reduce(grank[:], cmp_gt[:].rearrange("p j (g h) -> p (j g) h", g=NG), AX.X, ALU.add))
                after(n)
                n = step(dve.tensor_scalar(gmask[:], grank[:], float(TOP_G), None, ALU.is_lt))
                after(n)
                gm = bc(gmask[:].unsqueeze(2), [P, NB * NG, GS])
                mk = masked[:].rearrange("p j (g e) -> p (j g) e", g=NG)
                n = step(dve.tensor_tensor(mk, score[:].rearrange("p j (g e) -> p (j g) e", g=NG), gm, ALU.mult))
                after(n)
                n = step(dve.scalar_tensor_tensor(mk, gm, -1.0, mk, ALU.add, ALU.add))
                after(n)

            def top_():
                for j in range(NB):
                    n = step(dve.max(topv[:, j], masked[:, j]))
                for j in range(NB):
                    after(n - NB + 1 + j)
                    m = step(dve.max_index(topi[:, j], topv[:, j], masked[:, j]))
                after(m)

            def mask():
                n = step(dve.tensor_copy(posk[:].rearrange("p (j k) -> p j k", k=TOP), topi[:, :, 0:TOP]))
                after(n)
                n = step(dve.tensor_tensor(onehot[:], bc(iota_row[:, 0:E].unsqueeze(1), [P, NB * TOP, E]),
                                           bc(posk[:].unsqueeze(2), [P, NB * TOP, E]), ALU.is_equal))
                after(n)
                oh = onehot[:].rearrange("p (j k) e -> p j e k", k=TOP)
                with nc.allow_low_precision(reason="counts of 0 or 1"):
                    dve.tensor_reduce(mask_bf[:].rearrange("p (j e) -> p j e", e=E), oh, AX.X, ALU.add).then_inc(mask_ready, 1)

            def ranks():
                n = step(dve.memset(reset[:], 1.0))
                after(n)
                step(dve.memset(reset[:, :, 0], 0.0))
                dve.wait_ge(ranks_ready, 1)
                n = step(dve.tensor_copy(total[:], pk[2][:, 0:NB * E].rearrange("p (j e) -> p e j", e=E)))
                after(n)
                flat = "p e j -> p (e j)"
                n = step(dve.tensor_tensor_scan(cmp_gt[:].rearrange(flat), reset[:].rearrange(flat), total[:].rearrange(flat), 0.0,
                                                ALU.mult, ALU.add))
                after(n)

            def blocks():
                counts_ = cmp_gt[:][:, :, NB - 1]
                n = step(dve.tensor_tensor(cmp_eq[:], bc(counts_.unsqueeze(2), [P, E, NB]), bc(steps[:].unsqueeze(1), [P, E, NB]), ALU.is_gt))
                after(n)
                n = step(dve.tensor_reduce(nblk[:], cmp_eq[:], AX.X, ALU.add))
                after(n)
                n = step(dve.tensor_tensor_scan(bend[:], ones[:, 0:E], nblk[:], 0.0, ALU.mult, ALU.add))
                after(n)
                n = step(dve.tensor_tensor(bstart[:], bend[:], nblk[:], ALU.subtract))
                m = step(dve.tensor_tensor(picked[0:1, 0:BW // 2],
                                           bc(iota_row[0:1, 0:BW // 2].unsqueeze(2), [1, BW // 2, E]),
                                           bc(bend[0:1].unsqueeze(1), [1, BW // 2, E]), ALU.is_ge))
                after(m)
                m = step(dve.tensor_reduce(slotf[:, 0:BW // 2], picked[0:1, 0:BW // 2], AX.X, ALU.add))
                after(m)
                m = step(dve.tensor_tensor(picked[0:1, 0:BW // 2],
                                           bc(iota_row[0:1, BW // 2:BW].unsqueeze(2), [1, BW // 2, E]),
                                           bc(bend[0:1].unsqueeze(1), [1, BW // 2, E]), ALU.is_ge))
                after(m)
                m = step(dve.tensor_reduce(slotf[:, BW // 2:BW], picked[0:1, 0:BW // 2], AX.X, ALU.add))
                after(m)
                m = step(dve.tensor_scalar(slotf[:], slotf[:], float(E - 1), float(NS), ALU.min, ALU.add))
                after(m)
                m = step(dve.tensor_copy(block_slot[:], slotf[:]))

            def places():
                m = step(dve.tensor_tensor(cmp_gt[:], cmp_gt[:], total[:], ALU.subtract))
                after(m)
                m = step(dve.tensor_tensor(pos[:], pk[0][:, 0:NB * E].rearrange("p (j e) -> p j e", e=E),
                                           cmp_gt[:].rearrange("p e j -> p j e"), ALU.add))
                after(m)
                m = step(dve.scalar_tensor_tensor(pos[:], bc(bstart[:].unsqueeze(1), [P, NB, E]), float(P), pos[:], ALU.mult, ALU.add))
                after(m)
                m = step(dve.tensor_tensor(picked[:].rearrange("p (j k) e -> p j k e", k=TOP),
                                           onehot[:].rearrange("p (j k) e -> p j k e", k=TOP),
                                           bc(pos[:].unsqueeze(2), [P, NB, TOP, E]), ALU.mult))
                after(m)
                m = step(dve.tensor_reduce(posk[:], picked[:], AX.X, ALU.add))
                after(m)
                m = step(dve.tensor_copy(posi[:], posk[:]))
                after(m)
                step(dve.tensor_scalar(blki[:], posi[:], 7, None, ALU.arith_shift_right))
                m = step(dve.tensor_scalar(placei[:], posi[:], P - 1, None, ALU.bitwise_and))
                after(m)
                step(dve.tensor_copy(blkf[:], blki[:]))
                m = step(dve.tensor_copy(placef[:], placei[:]))
                after(m)

            def lists(k):
                for j in range(NB):
                    n = k * NB + j
                    at = j * TOP + k
                    need(dve, hot_used, n - RING + 1)
                    dve.tensor_scalar(hot_q[:, n % RING], iota_row[:], placef[:, at:at + 1], None, ALU.is_equal)
                    dve.tensor_scalar(hot_blk[:, n % RING], iota_row[:, 0:BW], blkf[:, at:at + 1], token_1[:, j:j + 1],
                                      ALU.is_equal, ALU.mult).then_inc(hot_ready, 1)

            def rows():
                dve.wait_ge(hot_used, NB * TOP)
                n = step(dve.tensor_copy(listed[:].rearrange("p k b -> p (k b)"), pk[7][:, 0:TOP * BW]))
                after(n)
                step(dve.tensor_scalar(filled[:], listed[:], 0.5, None, ALU.is_gt))
                n = step(dve.tensor_reduce(tok[:], listed[:].rearrange("p k b -> p b k"), AX.X, ALU.add))
                after(n)
                a1 = step(dve.scalar_tensor_tensor(kth[:], filled[:, 2], 2.0, filled[:, 1], ALU.mult, ALU.add))
                step(dve.tensor_scalar(empty[:], tok[:], 0.5, PAD, ALU.is_lt, ALU.mult))
                a2 = step(dve.tensor_scalar(rows_f[:], tok[:], -1.0, 0.0, ALU.add, ALU.max))
                after(a2)
                a2 = step(dve.tensor_copy(rows_in[:], rows_f[:]))
                after(a1)
                a1 = step(dve.scalar_tensor_tensor(kth[:], filled[:, 3], 3.0, kth[:], ALU.mult, ALU.add))
                after(a1)
                a1 = step(dve.scalar_tensor_tensor(kth[:], kth[:], float(NT), tok[:], ALU.mult, ALU.add))
                after(a1)
                a1 = step(dve.scalar_tensor_tensor(kth[:], kth[:], -1.0, empty[:], ALU.add, ALU.add))
                after(a1)
                a1 = step(dve.tensor_copy(rows_out[:], kth[:]))
                after(a1)
                dve.sem_inc(rows_ready, 1)
                dve.sem_inc(route_done, 1)

            for what, *a in order:
                if what in ("ln1", "ln2"):
                    norms(what, a[0])
                elif what == "router":
                    g, b = a
                    if b < GB:
                        x_lo_part("s", GB * g + b, s_x_lo[:, b], s_x_hi[:, b], pk[7])
                elif what == "ffn":
                    ffn(a[0])
                elif what == "lists":
                    lists(a[0])
                    if a[0] == TOP - 1:
                        rows()
                elif what == "scores":
                    scores()
                elif what == "top":
                    top_()
                elif what == "mask":
                    mask()
                elif what == "ranks":
                    ranks()
                elif what == "blocks":
                    blocks()
                elif what == "places":
                    places()
                elif what not in ("key", "split"):
                    recurrence(what, a[0])
            add_z(NB - 1)
            for slot in range(SL - LAST, SL):
                dve.wait_ge(whi_ready, 2 * (slot + 1))
                dve.tensor_tensor(w13_lo[:, slot], w13_raw[:, slot], f32(w13_hi[:, slot]), ALU.subtract).then_inc(wlo_last, 1)
                dve.tensor_tensor(w2_lo[0:IH, slot], w2_raw[0:IH, slot], f32(w2_hi[0:IH, slot]), ALU.subtract).then_inc(wlo_last, 1)

            def turn(i, u, has, m):
                if has(-1):
                    x_lo_part("r", i + 1, x_lo[:, (u + 1) % 2], x_hi[:, (u + 1) % 2], pk[(u + 1) % 2])
                if has(1):
                    dve.wait_ge(FF["r", "silu_ready"], i)
                    dve.tensor_tensor(h[:, (u - 1) % 4], h[:, (u - 1) % 4], pk[4 + (u - 1) % 2][:, I:2 * I], ALU.mult
                                      ).then_inc(FF["r", "h_ready"], 1)
                if has(3):
                    h_lo_part("r", i - 3, u - 3, HT[(u - 3) % 2])

            run_blocks(dve, turn)
            dve.wait_ge(z_added, NB)
            last = {}
            for n_ in range(NB // 2):
                dve.wait_ge(pairs_loaded[n_], 16 * TOP)
                for k in range(TOP):
                    for j in (2 * n_, 2 * n_ + 1):
                        if k:
                            after(last[j])
                        i = dve.scalar_tensor_tensor(base[:, j], pairs_in[:, k, j], topv[:, j, k:k + 1], base[:, j],
                                                     ALU.mult, ALU.add)
                        if k == TOP - 1:
                            i.then_inc(summed, 1)
                        else:
                            last[j] = step(i)


_INS = ["x", "ctx", "decay", "first", "wg", "w13", "w2"]


def kernel(x, ctx_2048, L0_xattn_time_decay, L0_xattn_time_first, L0_ffn_Wg, L0_ffn_W1, L0_ffn_W3, L0_ffn_W2,
           L0_ffn_Ws1, L0_ffn_Ws3, L0_ffn_Ws2):
    import concourse.bacc as _bacc
    from concourse.bass_utils import run_bass_kernel_spmd as _run

    a = {k: np.asarray(t) for k, t in dict(x=x, ctx=ctx_2048, decay=L0_xattn_time_decay, first=L0_xattn_time_first,
                                           wg=L0_ffn_Wg, w1=L0_ffn_W1, w3=L0_ffn_W3, w2=L0_ffn_W2, s1=L0_ffn_Ws1,
                                           s3=L0_ffn_Ws3, s2=L0_ffn_Ws2).items()}
    w1 = np.concatenate([a["s1"].reshape(NS, I, C), a["w1"]])
    w3 = np.concatenate([a["s3"].reshape(NS, I, C), a["w3"]])
    w2 = np.concatenate([a["s2"].reshape(C, NS, I).transpose(1, 0, 2), a["w2"]])
    w13 = np.concatenate([w1, w3], axis=1)
    arrays = {
        "x": a["x"],
        "ctx": a["ctx"].reshape(G, GB, P, 2, P).transpose(4, 0, 3, 1, 2).reshape(P, G, 2, N),
        "decay": a["decay"].reshape(2, P).T, "first": a["first"].reshape(2, P).T,
        "wg": a["wg"].reshape(E, 2, P).transpose(2, 1, 0),
        "w13": w13.reshape(NS + E, 2 * I, 2, P).transpose(3, 0, 2, 1),
        "w2": w2.reshape(NS + E, C, 2, IH).transpose(3, 0, 2, 1),
    }
    nc = _bacc.Bacc("TRN2", target_bir_lowering=False, num_devices=1)
    data, args = {}, []
    for name in _INS:
        t = np.ascontiguousarray(arrays[name])
        data[f"in_{name}_dram"] = t
        args.append(nc.dram_tensor(f"in_{name}_dram", t.shape, mybir.dt.from_np(t.dtype), kind="ExternalInput").ap())
    o = nc.dram_tensor("out_0_dram", (NB, P, C), F32, kind="ExternalOutput").ap()
    xattn_moe_kernel(nc, *args, o)
    r = _run(nc, [data], core_ids=[0])
    return r.results[0]["out_0_dram"]
```

```python
from contextlib import ExitStack

import numpy as np

import concourse.bass as bass
from concourse import mybir

ALU = mybir.AluOpType
ACT = mybir.ActivationFunctionType
AX = mybir.AxisListType
F32 = mybir.dt.float32
F32R = mybir.dt.float32r
BF16 = mybir.dt.bfloat16
F16 = mybir.dt.float16
I32 = mybir.dt.int32
U32 = mybir.dt.uint32

P = 128
NB = 16
C = 256
NT = NB * P
E = 16
NS = 2
NG, GS = 4, 4
TOP, TOP_G = 4, 2
I = 176
IH = I // 2
GB = 4
G = NB // GB
N = GB * P
BLK = NT * TOP // P + E - 1
BW = BLK + 1
LATE = 9
LAST = 3
NEG = -1e38
EPS = 1e-5
PAD = 100000.0


def ds(start, size):
    return bass.ds(start, size)


def xattn_moe_kernel(nc, x, ctx, decay, first, wg, w13, w2, out):
    xhat_dram = nc.dram_tensor("xhat_rows", [NT, C], F32, kind="Internal").ap()
    pair_dram = nc.dram_tensor("pair_rows", [TOP * NT, C], F32, kind="Internal").ap()
    x_t = x.rearrange("b t c -> t b c")
    out_t = out.rearrange("b t c -> t b c")
    xhat_t = xhat_dram.rearrange("(j p) c -> p j c", p=P)
    pair_t = pair_dram.rearrange("(k j p) c -> p k j c", p=P, k=TOP)

    with ExitStack() as stack:
        top = [(nc.sbuf_base + 63) // 64 * 64]

        def place(name, shape, dt, at=None):
            size = int(np.prod(shape[1:])) * mybir.dt.size(dt)
            size = (size + 31) // 32 * 32
            where = top if at is None else at
            t = nc.alloc_sbuf_tensor_at(name, shape, dt, offset=where[0])
            where[0] += size
            return t

        SL = NS + E
        here = [top[0]]
        w13_hi = place("w13_hi", [P, SL, 2, 2 * I], F32R)
        at_lo13 = [top[0]]
        w13_lo = place("w13_lo", [P, SL, 2, 2 * I], F32R)
        at_hi2 = [top[0]]
        w2_hi = place("w2_hi", [P, SL, 2, C], F32R)
        at_lo2 = [top[0]]
        w2_lo = place("w2_lo", [P, SL, 2, C], F32R)
        w13_raw = place("w13_raw", [P, SL, 2, 2 * I], F32, [at_lo13[0]])
        w2_raw = place("w2_raw", [P, SL, 2, C], F32, [at_lo2[0]])
        early13 = (SL - LATE) * 2 * 2 * I * 4
        early2 = (SL - LATE) * 2 * C * 4
        z1, z2 = [here[0] + early13], [at_lo13[0] + early13]
        z3, z4 = [at_hi2[0] + early2], [at_lo2[0] + early2]

        base = place("base", [P, NB, C], F32)
        at_x = [top[0]]
        s_x_hi = place("s_x_hi", [P, GB, 2, P], F32R)
        s_x_lo = place("s_x_lo", [P, GB, 2, P], F32R)
        x_hi = place("x_hi", [P, 2, 2, P], F32R, at_x)
        x_lo = place("x_lo", [P, 2, 2, P], F32R, at_x)
        g_rows = place("g_rows", [P, 4, C], F32, at_x)
        h = place("h", [P, 4, I], F32)
        h_hi = place("h_hi", [P, 2, 2, P], F32R)
        h_lo = place("h_lo", [P, 2, 2, P], F32R)
        ident = place("ident", [P, P], F32)
        topv = place("topv", [P, NB, 8], F32)
        rows_in = place("rows_in", [P, BW], I32)
        rows_out = place("rows_out", [P, BW], I32)
        block_slot = place("block_slot", [1, BW], I32)
        token_1 = place("token_1", [P, NB], F32)
        lower = place("lower", [P, NG, NG], F32)
        at_y = [top[0]]
        wg_parts = place("wg_parts", [P, 2, 2 * E], F32R, at_y)
        logits = place("logits", [P, NB, E], F32, at_y)
        before = place("before", [P, P], BF16, at_y)
        ones = place("ones", [P, P], BF16, at_y)
        iota_row = place("iota_row", [P, P], F16, at_y)
        steps = place("steps", [P, NB], F16, at_y)
        y_rows = place("y_rows", [P, 4, C], F32)
        assert at_y[0] <= top[0]
        assert top[0] <= nc.sbuf_usable_end, (top[0], nc.sbuf_usable_end)

        x_in = place("x_in", [P, 3, GB, C], F32, z1)
        v_in = place("v_in", [P, 2, 2, N], F32, z1)
        wkv_d = place("wkv_d", [P, N], F32, z1)
        k_c = place("k_c0", [P, N], F32, z1), place("k_c1", [P, N], F32, z2)
        clamp_pos = place("clamp_pos0", [P, 2, N], F32, z2), place("clamp_pos1", [P, 2, N], F32, z4)
        clamp_neg = place("clamp_neg0", [P, 2, N], F32, z2), place("clamp_neg1", [P, 2, N], F32, z4)
        kv = place("kv0", [P, 2, N], F32, z2), place("kv1", [P, 2, N], F32, z4)
        k_t = place("k_t", [P, GB, C], F32, z2)
        decay_row = place("decay_row", [P, 2, N], F32, z2)
        num = place("num0", [P, N], F32, z2), place("num1", [P, N], F32, z4)
        xhat = place("xhat", [P, GB, C], F32, z3)
        den = place("den", [P, N], F32, z3)
        pp = place("pp0", [P, N + 1], F32, z3), place("pp1", [P, N + 1], F32, z3)
        aa = place("aa", [P, N + 1], F32, z3)
        bb = place("bb", [P, N + 1], F32, z3)
        wg_raw = place("wg_raw", [P, 2, E], F32, z3)
        td = place("td", [P, 2], F32, z3)
        tf = place("tf", [P, 2], F32, z3)
        wdec = place("wdec", [P, 2], F32, z3)
        wneg = place("wneg", [P, 2], F32, z3)
        uneg = place("uneg", [P, 2], F32, z3)
        stats = place("stats", [P, GB, 6], F32, z3)
        mv = place("mv", [P, GB, 2], F32, z3), place("mv2", [P, GB, 2], F32, z3)
        vpe = place("vpe", [P, GB], F32, z3)
        rstd = place("rstd", [P, GB], F32, z3), place("rstd2", [P, GB], F32, z3)
        shift = place("shift", [P, GB], F32, z3), place("shift2", [P, GB], F32, z3)
        half_neg = place("half_neg", [P, GB], F32, z3)
        assert z1[0] <= here[0] + SL * 4 * I * 4 and z2[0] <= at_lo13[0] + SL * 4 * I * 4
        assert z3[0] <= at_hi2[0] + SL * 2 * C * 4 and z4[0] <= at_lo2[0] + SL * 2 * C * 4, z4

        last13, last2 = LAST * 4 * I * 4, LAST * 2 * C * 4
        RING = 16
        t1 = [here[0] + SL * 4 * I * 4 - last13]
        hot_q = place("hot_q", [P, RING, P], F16, t1)
        hot_blk = place("hot_blk", [P, RING, BW], F16, t1)
        blkf = place("blkf", [P, NB * TOP], F32, t1)
        placef = place("placef", [P, NB * TOP], F32, t1)
        tok = place("tok", [P, BW], F32, t1)
        kth = place("kth", [P, BW], F32, t1)
        rows_f = place("rows_f", [P, BW], F32, t1)
        empty = place("empty", [P, BW], F32, t1)
        t3 = [at_hi2[0] + SL * 2 * C * 4 - last2]
        listed = place("listed", [P, TOP, BW], F32, t3)
        filled = place("filled", [P, TOP, BW], F32, t3)
        slotf = place("slotf", [1, BW], F32, t3)
        score = place("score", [P, NB, E], F32, t3)
        cmp_gt = place("cmp_gt", [P, NB, E], F32, t3)
        t3b = [t3[0]]
        masked = place("masked", [P, NB, E], F32, t3)
        nblk = place("nblk", [P, E], F32, t3b)
        bend = place("bend", [P, E], F32, t3b)
        bstart = place("bstart", [P, E], F32, t3b)
        bend_of = place("bend_of", [P, 1], F32, t3b)
        ended = place("ended", [E, BW], BF16, t3b)
        tmax = place("tmax", [P, NB], F32, t3)
        tsum = place("tsum", [P, NB], F32, t3)
        trec = place("trec", [P, NB], F32, t3)
        t2 = [at_lo13[0] + SL * 4 * I * 4 - last13]
        t2b = [t2[0]]
        onehot = place("onehot", [P, NB * TOP, E], F32, t2)
        grank = place("grank", [P, NB * NG], F32, t2b)
        gmask = place("gmask", [P, NB * NG], F32, t2b)
        picked = place("picked", [P, NB * TOP, E], F32, t2)
        grp = place("grp", [P, NB * NG], F32, t2)
        t4 = [at_lo2[0] + SL * 2 * C * 4 - last2]
        cmp_eq = place("cmp_eq", [P, NB, E], F32, t4)
        total = place("total", [P, E, NB], F32, t4)
        pos = place("pos", [P, NB, E], F32, t4)
        reset = place("reset", [P, E, NB], F32, t4)
        topi = place("topi", [P, NB, 8], U32, t4)
        posk = place("posk", [P, NB * TOP], F32, t4)
        posi = place("posi", [P, NB * TOP], I32, t4)
        blki = place("blki", [P, NB * TOP], I32, t4)
        placei = place("placei", [P, NB * TOP], I32, t4)
        mask_bf = place("mask_bf", [P, NB * E], BF16, t4)
        assert t1[0] <= here[0] + SL * 4 * I * 4 and t2[0] <= at_lo13[0] + SL * 4 * I * 4
        assert t3[0] <= at_hi2[0] + SL * 2 * C * 4 and t4[0] <= at_lo2[0] + SL * 2 * C * 4, (t3, t4)
        pairs_in = place("pairs_in", [P, TOP, NB, C], F32, [here[0]])
        pk = [stack.enter_context(nc.psum_tensor(f"bank{i}", [P, 512], F32)) for i in range(8)]

        def sem(name):
            return stack.enter_context(nc.semaphore(name))

        def need(eng, s, count):
            if not isinstance(count, int) or count > 0:
                eng.wait_ge(s, count)

        x_loaded = [sem(f"x_loaded{i}") for i in range(3)]
        ctx_loaded = [sem(f"ctx_loaded{i}") for i in range(2)]
        small_loaded = sem("small_loaded")
        CHUNKS = [(0, 2), (2, 5), (5, SL - LATE), (SL - LATE, SL - LAST), (SL - LAST, SL)]
        w_loaded = [sem(f"w_loaded{i}") for i in range(len(CHUNKS))]
        xhat_stored = sem("xhat_stored")
        out_stored = sem("out_stored")
        pairs_loaded = [[sem(f"pairs_loaded{i}_{k}") for k in range(TOP)] for i in range(NB // 2)]
        consts_ready = sem("consts_ready")
        pool_const = sem("pool_const")
        decay_exp = sem("decay_exp")
        stats_ready = sem("stats_ready")
        mv1_ready, rstd1_ready = sem("mv1_ready"), sem("rstd1_ready")
        mv2_ready, rstd2_ready = sem("mv2_ready"), sem("rstd2_ready")
        kt_ready = sem("kt_ready")
        kT_ready, k_ready = sem("kT_ready"), sem("k_ready")
        pp_ready, d_raw, d_ready = sem("pp_ready"), sem("d_raw"), sem("d_ready")
        clamp_ready, exp_ready, kv_ready = sem("clamp_ready"), sem("exp_ready"), sem("kv_ready")
        kv_used = sem("kv_used")
        wkv_ready, yT_ready, x1_ready = sem("wkv_ready"), sem("yT_ready"), sem("x1_ready")
        xhat_ready = sem("xhat_ready")
        FF = {}
        for kind in ("s", "r"):
            for what in ("xT_ready", "xhi_ready", "xlo_ready", "h13_ready", "silu_ready", "h_ready", "hT_ready",
                         "hhi_ready", "hlo_ready", "y_ready"):
                FF[kind, what] = sem(f"{kind}_{what}")
        logits_ready, logits_copied, z_added, gated = sem("logits_ready"), sem("logits_copied"), sem("z_added"), sem("gated")
        wg_split = sem("wg_split")
        whi_ready, wlo_ready, wlo_last = sem("whi_ready"), sem("wlo_ready"), sem("wlo_last")
        vstep = sem("vstep")
        pstep = sem("pstep")
        shifted, scores_exp = sem("shifted"), sem("scores_exp")
        ended_ready, ended_counted = sem("ended_ready"), sem("ended_counted")
        mask_ready, ranks_ready = sem("mask_ready"), sem("ranks_ready")
        places_ready, hot_ready, hot_pool_ready = sem("places_ready"), sem("hot_ready"), sem("hot_pool_ready")
        hot_used = sem("hot_used")
        rows_ready = sem("rows_ready")
        gathered = [sem(f"gathered{i}") for i in range(4)]
        y_staged = sem("y_staged")
        scattered = [sem(f"scattered{i}") for i in range(4)]
        summed = sem("summed")

        block = stack.enter_context(nc.Block())

        HS = 2 * G
        UNITS = NB * NS

        def f32(ap):
            return ap.bitcast(F32)

        def by_pool(j):
            return j % 5 in (2, 4)

        def x_bank(g, b):
            return pk[7] if g < G - 1 else (pk[0], pk[2])[b % 2]

        POOL_TILES = [j for j in range(NB) if by_pool(j)]

        LATE_SPLIT = {"scores": 0, "top": 1, "mask": 2, "ranks": 3, "blocks": 4, "places": 5}
        assert len(LATE_SPLIT) == LATE - LAST

        def first_part():
            done, allowed = [0], [0]

            def units(count):
                for _ in range(count):
                    if done[0] < allowed[0]:
                        yield "ffn", done[0]
                        done[0] += 1

            def turn(g, b):
                yield from units(NS * (GB * (g - 1) + b + 1) - done[0])
                yield "turn", g, b

            def low(g, b):
                yield "low", g, b
                yield "logits", g, b
                allowed[0] = NS * (GB * g + b + 1)

            yield from [("ln1", 0), ("kt", 0), ("key", 0), ("key", 1), ("max", 0), ("clamp", 0), ("max", 1), ("kv", 0)]
            yield from [("clamp", 1), ("ln1", 1), ("kt", 1), ("kv", 1), ("split", 0)]
            yield "key", 2
            for s in range(HS):
                g, odd, ahead = s // 2, s % 2, s + 2 < HS
                yield "sums", s
                if s:
                    yield "x1", s - 1
                if g and odd:
                    yield from low(g - 1, 1)
                    yield from turn(g - 1, 2)
                if g and not odd:
                    yield "ln2", g - 1
                if ahead:
                    yield "max", s + 2
                if s + 1 < SL - LATE:
                    yield "split", s + 1
                if g and not odd:
                    yield "xhat", g - 1
                yield from units(1)
                yield "ratio", s
                if g and not odd:
                    yield from turn(g - 1, 0)
                if g and odd:
                    yield from low(g - 1, 2)
                    yield from turn(g - 1, 3)
                if odd and g + 2 < G:
                    yield "ln1", g + 2
                yield from units(1)
                if ahead:
                    yield "clamp", s + 2
                    yield "kv", s + 2
                yield "recip", s
                yield "wkv", s
                if g and odd:
                    yield from low(g - 1, 3)
                yield from units(1)
                yield "back", s
                if g and not odd:
                    yield from low(g - 1, 0)
                    yield from turn(g - 1, 1)
                if g and odd:
                    yield "gather", g - 1
                if odd and g + 2 < G:
                    yield "kt", g + 2
                if s + 3 < HS:
                    yield "key", s + 3
                yield from units(1)
            yield "x1", HS - 1
            yield "ln2", G - 1
            yield from units(2)
            yield "xhat", G - 1
            yield from units(1)
            for b in range(2):
                yield from turn(G - 1, b)
            for b in range(GB):
                yield from low(G - 1, b)
                if b + 2 < GB:
                    yield from turn(G - 1, b + 2)
            yield "gather", G - 1
            allowed[0] = UNITS + 4
            for part in ("scores", "top", "mask", "ranks", "blocks", "places"):
                yield part,
                yield from units(1)
            for k in range(TOP):
                yield "lists", k
                yield from units(1)
            yield from units(UNITS)

        order = list(first_part())

        @block.sync
        def _(sp):
            def load_x(g):
                if g >= 3:
                    sp.wait_ge(x1_ready, 2 * (g - 2))
                sp.dma_start(x_in[:, g % 3], x_t[:, g * GB:(g + 1) * GB, :]).then_inc(x_loaded[g % 3], 16)

            def load_ctx(g):
                if g >= 2:
                    sp.wait_ge(kv_ready, 2 * (g - 1))
                sp.dma_start(v_in[:, g % 2], ctx[:, g]).then_inc(ctx_loaded[g % 2], 16)

            def load_weights(n):
                a, b = CHUNKS[n]
                sp.dma_start(w13_raw[:, a:b], w13[:, a:b]).then_inc(w_loaded[n], 16)
                sp.dma_start(w2_raw[0:IH, a:b], w2[:, a:b]).then_inc(w_loaded[n], 16)

            load_x(0)
            sp.dma_start(td[:], decay).then_inc(small_loaded, 16)
            sp.dma_start(tf[:], first).then_inc(small_loaded, 16)
            sp.dma_start(wg_raw[:], wg).then_inc(small_loaded, 16)
            load_ctx(0)
            load_x(1)
            load_weights(0)
            load_ctx(1)
            load_x(2)
            load_weights(1)
            load_weights(2)
            load_ctx(2)
            load_x(3)
            for g in range(G):
                if g == G - 1:
                    sp.wait_ge(yT_ready, HS)
                    load_weights(3)
                sp.wait_ge(xhat_ready, GB * (g + 1))
                sp.dma_start(xhat_t[:, g * GB:(g + 1) * GB, :], xhat[:]).then_inc(xhat_stored, 16)
                if g == 0:
                    load_ctx(3)
            sp.wait_ge(places_ready, 1)
            load_weights(4)
            sp.wait_ge(FF["r", "y_ready"], BLK)
            for i in range(4):
                sp.wait_ge(scattered[i], 16 * ((BLK + 3 - i) // 4))
            for n in range(NB // 2):
                for k in range(TOP):
                    sp.dma_start(pairs_in[:, k, 2 * n:2 * n + 2], pair_t[:, k, 2 * n:2 * n + 2]).then_inc(pairs_loaded[n][k], 16)
            for n in range(NB // 2):
                sp.wait_ge(summed, 2 * n + 2)
                sp.dma_start(out_t[:, 2 * n:2 * n + 2], base[:, 2 * n:2 * n + 2]).then_inc(out_stored, 16)
            sp.wait_ge(out_stored, 16 * (NB // 2))

        @block.gpsimd
        def _(pool):
            steps_done = [0]

            def step(ins):
                steps_done[0] += 1
                ins.then_inc(pstep, 1)
                return steps_done[0]

            step(pool.memset(ident[:], 0.0))
            step(pool.memset(before[:], 1.0))
            step(pool.memset(lower[:], 1.0))
            pool.memset(half_neg[:], -0.5).then_inc(pool_const, 1)
            pool.memset(ones[:], 1.0).then_inc(consts_ready, 1)
            pool.iota(iota_row[:], [[1, P]], base=0, channel_multiplier=0,
                      allow_small_or_imprecise_dtypes=True).then_inc(consts_ready, 1)
            pool.iota(token_1[:], [[P, NB]], base=1, channel_multiplier=1,
                      allow_small_or_imprecise_dtypes=True).then_inc(consts_ready, 1)
            pool.iota(steps[:], [[P, NB]], base=0, channel_multiplier=0,
                      allow_small_or_imprecise_dtypes=True).then_inc(consts_ready, 1)
            pool.wait_ge(pstep, 3)
            pool.affine_select(out=ident[:], in_=ident[:], compare_op=ALU.not_equal, fill=1.0, base=0,
                               pattern=[[-1, P]], channel_multiplier=1).then_inc(consts_ready, 1)
            pool.affine_select(out=before[:], in_=before[:], compare_op=ALU.is_gt, fill=0.0, base=0,
                               pattern=[[1, P]], channel_multiplier=-1).then_inc(consts_ready, 1)
            pool.affine_select(out=lower[:], in_=lower[:], compare_op=ALU.is_gt, fill=0.0, base=0,
                               pattern=[[1, NG], [-1, NG]], channel_multiplier=0).then_inc(consts_ready, 1)
            pool.wait_ge(pool_const, 1)

            def power(l, g, ready, done):
                pool.wait_ge(ready, g + 1)
                n = step(pool.tensor_scalar(vpe[:], mv[l][:, :, 1], EPS, None, ALU.add))
                pool.wait_ge(pstep, n)
                need(pool, (kt_ready, xhat_ready)[l], GB * g)
                n = step(pool.tensor_tensor(rstd[l][:], vpe[:], half_neg[:], ALU.pow))
                pool.wait_ge(pstep, n)
                n = step(pool.tensor_tensor(shift[l][:], mv[l][:, :, 0], rstd[l][:], ALU.mult))
                pool.wait_ge(pstep, n)
                pool.tensor_scalar(shift[l][:], shift[l][:], -1.0, None, ALU.mult).then_inc(done, 1)

            def split_lo(slot):
                pool.wait_ge(whi_ready, 2 * (slot + 1))
                pool.tensor_tensor(w13_lo[:, slot], w13_raw[:, slot], f32(w13_hi[:, slot]), ALU.subtract).then_inc(wlo_ready, 1)
                pool.tensor_tensor(w2_lo[0:IH, slot], w2_raw[0:IH, slot], f32(w2_hi[0:IH, slot]), ALU.subtract).then_inc(wlo_ready, 1)

            for what, *a in order:
                if what == "ln1":
                    power(0, a[0], mv1_ready, rstd1_ready)
                elif what == "ln2":
                    power(1, a[0], mv2_ready, rstd2_ready)
                elif what == "max":
                    s = a[0]
                    pool.wait_ge(pp_ready, s + 1)
                    need(pool, clamp_ready, s)
                    pool.tensor_tensor(wkv_d[:], pp[s % 2][:, 0:N], k_c[s % 2][:], ALU.subtract).then_inc(d_raw, 1)
                    pool.wait_ge(d_raw, s + 1)
                    pool.memset(wkv_d[:, 0:N:P], NEG).then_inc(d_ready, 1)
                elif what == "kv":
                    s = a[0]
                    pool.wait_ge(exp_ready, 2 * (s + 1))
                    pool.wait_ge(ctx_loaded[s // 2 % 2], 16 * (s // 4 + 1))
                    need(pool, kv_used, s - 1)
                    pool.tensor_tensor(kv[s % 2][:], clamp_pos[s % 2][:],
                                       v_in[:, s // 2 % 2, s % 2].unsqueeze(1).broadcast_to([P, 2, N]),
                                       ALU.mult).then_inc(kv_ready, 1)
                elif what == "split":
                    split_lo(a[0])
                elif what in LATE_SPLIT:
                    split_lo(SL - LATE + LATE_SPLIT[what])
                elif what == "lists":
                    k = a[0]
                    pool.wait_ge(places_ready, 1)
                    for j in range(NB):
                        n = k * NB + j
                        at = j * TOP + k
                        if not by_pool(j):
                            continue
                        need(pool, hot_used, n - RING + 1)
                        pool.tensor_scalar(hot_blk[:, n % RING], iota_row[:, 0:BW], blkf[:, at:at + 1], token_1[:, j:j + 1],
                                           ALU.is_equal, ALU.mult).then_inc(hot_pool_ready, 1)
            pool.wait_ge(FF["s", "h13_ready"], UNITS)
            pool.wait_ge(xhat_stored, 16 * G)
            pool.wait_ge(rows_ready, 1)

            def gather(i):
                need(pool, FF["r", "xT_ready"], i - 3)
                pool.indirect_dma_start(g_rows[:, i % 4, :], None, xhat_dram,
                                        bass.IndirectOffsetOnAxis(ap=rows_in[:, i:i + 1].bitcast(U32), axis=0)
                                        ).then_inc(gathered[i % 4], 16)

            AHEAD = 11
            for i in range(AHEAD):
                gather(i)
            for i in range(BLK):
                if i + AHEAD < BLK:
                    gather(i + AHEAD)
                pool.wait_ge(y_staged, i + 1)
                pool.indirect_dma_start(pair_dram, bass.IndirectOffsetOnAxis(ap=rows_out[:, i:i + 1].bitcast(U32), axis=0),
                                        y_rows[:, i % 4, :], None, bounds_check=TOP * NT - 1, oob_is_err=False
                                        ).then_inc(scattered[i % 4], 16)

        HT = pk[6], pk[3]
        YB = pk[7], pk[2]

        LEAD = 8

        def run_blocks(eng, turn, head=None):
            END = BLK + 4
            rounds = (BLK - 2 - LEAD) // 4

            def single(i):
                if head:
                    head(None, i)
                turn(i, i % 4, lambda d: 0 <= i - d < BLK, None)

            for i in range(-2, LEAD):
                single(i)
            with eng.Fori(0, rounds) as m:
                if head:
                    head(m, 4 * m + LEAD)
                for u in range(LEAD, LEAD + 4):
                    turn(4 * m + u, u, lambda d: True, m)
            for i in range(LEAD + 4 * rounds, END):
                single(i)

        @block.scalar
        def _(act):
            act.wait_ge(small_loaded, 48)
            act.activation(wneg[:], td[:], ACT.Exp).then_inc(decay_exp, 1)
            act.activation(wg_parts[:, :, 0:E], wg_raw[:], ACT.Copy).then_inc(wg_split, 1)

            def split_hi(slot):
                n = [n for n, (a, b) in enumerate(CHUNKS) if a <= slot < b][0]
                act.wait_ge(w_loaded[n], 32)
                act.activation(w13_hi[:, slot], w13_raw[:, slot], ACT.Copy).then_inc(whi_ready, 1)
                act.activation(w2_hi[0:IH, slot], w2_raw[0:IH, slot], ACT.Copy).then_inc(whi_ready, 1)

            def scale_rows(l, b, dst, src, done):
                act.activation(dst, src, ACT.Identity, bias=shift[l][:, b:b + 1], scale=rstd[l][:, b:b + 1]
                               ).then_inc(done, 1)

            for what, *a in order:
                s = a[0] if a else None
                if what == "kt":
                    act.wait_ge(rstd1_ready, s + 1)
                    need(act, kT_ready, 2 * s)
                    for b in range(GB):
                        scale_rows(0, b, k_t[:, b], x_in[:, s % 3, b], kt_ready)
                elif what == "xhat":
                    act.wait_ge(rstd2_ready, s + 1)
                    need(act, xhat_stored, 16 * s)
                    need(act, FF["s", "xT_ready"], GB * s)
                    for b in range(GB):
                        scale_rows(1, b, xhat[:, b], base[:, GB * s + b], xhat_ready)
                elif what == "key":
                    act.wait_ge(kT_ready, s + 1)
                    need(act, d_raw, s - 1)
                    act.activation(k_c[s % 2][:], pk[0][:], ACT.Copy).then_inc(k_ready, 1)
                elif what == "clamp":
                    act.wait_ge(d_ready, s + 1)
                    need(act, kv_used, s - 1)
                    for n, (over, under) in enumerate(((wdec, wneg), (uneg, tf))):
                        h_ = slice(s % 2, s % 2 + 1)
                        act.activation(clamp_pos[s % 2][:, n], wkv_d[:], ACT.Relu, bias=over[:, h_])
                        i = act.activation(clamp_neg[s % 2][:, n], wkv_d[:], ACT.Relu, bias=under[:, h_], scale=-1.0)
                    i.then_inc(clamp_ready, 1)
                    act.wait_ge(clamp_ready, s + 1)
                    act.activation(clamp_pos[s % 2][:], clamp_pos[s % 2][:], ACT.Exp, scale=-1.0).then_inc(exp_ready, 1)
                    act.activation(clamp_neg[s % 2][:], clamp_neg[s % 2][:], ACT.Exp, scale=-1.0).then_inc(exp_ready, 1)
                elif what == "split":
                    split_hi(s)
                elif what == "turn":
                    g, b = a
                    t = GB * g + b
                    act.wait_ge(FF["s", "xT_ready"], t + 1)
                    need(act, FF["s", "h13_ready"], 2 * (t - GB + 1))
                    act.activation(s_x_hi[:, b].rearrange("p c t -> p (c t)"), x_bank(g, b)[:, 0:2 * P], ACT.Copy
                                   ).then_inc(FF["s", "xhi_ready"], 1)
                elif what == "ffn":
                    n = s
                    if n < UNITS:
                        act.wait_ge(FF["s", "h13_ready"], n + 1)
                        need(act, FF["s", "hT_ready"], n - 3)
                        act.activation(h[:, n % 4], pk[4 + n % 2][:, 0:I], ACT.Tanh, scale=0.5).then_inc(FF["s", "silu_ready"], 1)
                    w = n - 2
                    if 0 <= w < UNITS:
                        act.wait_ge(FF["s", "hT_ready"], w + 1)
                        need(act, FF["s", "y_ready"], w - 1)
                        act.activation(h_hi[0:IH, w % 2].rearrange("p c t -> p (c t)"), HT[w % 2][0:IH, 0:2 * P],
                                       ACT.Copy).then_inc(FF["s", "hhi_ready"], 1)
                elif what == "scores":
                    act.wait_ge(shifted, 1)
                    act.activation(score[:], masked[:], ACT.Exp).then_inc(scores_exp, 1)
                    act.wait_ge(xhat_stored, 16 * G)
                    act.wait_ge(FF["s", "xT_ready"], NB)
                if what in LATE_SPLIT:
                    split_hi(SL - LATE + LATE_SPLIT[what])
            act.wait_ge(places_ready, 1)
            act.activation(lower[:, 0, 0:1], token_1[:, 0:1], ACT.Silu)
            act.wait_ge(rows_ready, 1)
            for slot in range(SL - LAST, SL):
                split_hi(slot)
            act.wait_ge(FF["s", "y_ready"], UNITS)

            def x_part(i, u):
                act.wait_ge(FF["r", "xT_ready"], i + 1)
                need(act, FF["r", "h13_ready"], i - 1)
                act.activation(x_hi[:, u % 2].rearrange("p c t -> p (c t)"), pk[u % 2][:, 0:2 * P], ACT.Copy
                               ).then_inc(FF["r", "xhi_ready"], 1)

            def turn(i, u, has, m):
                if has(0):
                    act.wait_ge(FF["r", "h13_ready"], i + 1)
                    need(act, FF["r", "hT_ready"], i - 3)
                    act.activation(h[:, u % 4], pk[4 + u % 2][:, 0:I], ACT.Silu).then_inc(FF["r", "silu_ready"], 1)
                if has(-2):
                    x_part(i + 2, u + 2)
                if has(2):
                    act.wait_ge(FF["r", "hT_ready"], i - 1)
                    need(act, FF["r", "y_ready"], i - 3)
                    act.activation(h_hi[0:IH, u % 2].rearrange("p c t -> p (c t)"), HT[u % 2][0:IH, 0:2 * P],
                                   ACT.Copy).then_inc(FF["r", "hhi_ready"], 1)
                if has(4):
                    act.wait_ge(FF["r", "y_ready"], i - 3)
                    need(act, scattered[u % 4], 16 * (i // 4 - 1 if m is None else m + u // 4 - 1))
                    act.activation(y_rows[:, u % 4], YB[u % 2][:, 0:C], ACT.Copy).then_inc(y_staged, 1)

            run_blocks(act, turn)

        @block.tensor
        def _(pe):
            pe.wait_ge(consts_ready, 7)

            def x_turn(kind, i, bank, rows):
                for c in range(2):
                    t = pe.transpose(bank[:, c * P:(c + 1) * P], rows[:, c * P:(c + 1) * P], ident[:])
                t.then_inc(FF[kind, "xT_ready"], 1)

            def products(out_, left_hi, left_lo, right_hi, right_lo):
                for c in range(2):
                    for n, (a, b) in enumerate(((left_hi, right_hi), (left_hi, right_lo), (left_lo, right_hi))):
                        m = pe.matmul(out_, a(c), b(c), start=(c == 0 and n == 0), stop=(c == 1 and n == 2))
                return m

            def h_turn(kind, b, bank):
                for c in range(2):
                    t = pe.transpose(bank[0:IH, c * P:(c + 1) * P], h[:, b, c * IH:(c + 1) * IH], ident[:])
                t.then_inc(FF[kind, "hT_ready"], 1)

            for what, *a in order:
                s = a[0] if a else None
                if what == "key":
                    pe.wait_ge(kt_ready, GB * (s // 2 + 1))
                    need(pe, k_ready, s)
                    for b in range(GB):
                        t = pe.transpose(pk[0][:, b * P:(b + 1) * P], k_t[:, b, (s % 2) * P:(s % 2 + 1) * P], ident[:])
                    t.then_inc(kT_ready, 1)
                elif what == "back":
                    pe.wait_ge(wkv_ready, s + 1)
                    need(pe, x1_ready, s)
                    for b in range(GB):
                        t = pe.transpose(pk[2][:, b * P:(b + 1) * P], num[s % 2][:, b * P:(b + 1) * P], ident[:])
                    t.then_inc(yT_ready, 1)
                elif what == "turn":
                    g, b = a
                    t = GB * g + b
                    pe.wait_ge(xhat_ready, t + 1)
                    need(pe, FF["s", "xlo_ready"], t if g < G - 1 else t - 1)
                    need(pe, logits_copied, GB * min(g, G - 2))
                    x_turn("s", t, x_bank(g, b), xhat[:, b])
                elif what == "logits":
                    g, b = a
                    pe.wait_ge(FF["s", "xlo_ready"], GB * g + b + 1)
                    pe.wait_ge(wg_split, 2)
                    need(pe, logits_copied, GB * g)
                    for c in range(2):
                        for m, l in enumerate((s_x_hi, s_x_lo)):
                            m_ = pe.matmul(pk[7][:, 2 * P + b * 2 * E:2 * P + (b + 1) * 2 * E], l[:, b, c],
                                           wg_parts[:, c], start=(c == 0 and m == 0), stop=(c == 1 and m == 1))
                    m_.then_inc(logits_ready, 1)
                elif what == "ffn":
                    n = s
                    if n < UNITS:
                        if n == 0:
                            pe.wait_ge(wlo_ready, 4)
                        need(pe, FF["s", "h_ready"], n - 1)
                        b = n // 2 % GB
                        products(pk[4 + n % 2][:, 0:2 * I], lambda c: s_x_hi[:, b, c], lambda c: s_x_lo[:, b, c],
                                 lambda c: w13_hi[:, n % 2, c], lambda c: w13_lo[:, n % 2, c]
                                 ).then_inc(FF["s", "h13_ready"], 1)
                    w = n - 4
                    if w >= 0:
                        pe.wait_ge(FF["s", "hlo_ready"], w + 1)
                        if w % 2 == 0:
                            need(pe, z_added, w // 2)
                        k = 0
                        for c in range(2):
                            for l, r in ((h_hi, w2_hi), (h_hi, w2_lo), (h_lo, w2_hi)):
                                m = pe.matmul(pk[1][:, 0:C], l[0:IH, w % 2, c], r[0:IH, w % 2, c],
                                              start=(w % 2 == 0 and k == 0), stop=(w % 2 == 1 and k == 5))
                                k += 1
                        m.then_inc(FF["s", "y_ready"], 1)
                    w = n - 2
                    if 0 <= w < UNITS:
                        pe.wait_ge(FF["s", "h_ready"], w + 1)
                        need(pe, FF["s", "hlo_ready"], w - 1)
                        h_turn("s", w % 4, HT[w % 2])
                elif what == "ranks":
                    pe.wait_ge(mask_ready, 1)
                    pe.matmul(pk[0][:, 0:NB * E], before[:], mask_bf[:], start=True, stop=True)
                    pe.matmul(pk[2][:, 0:NB * E], ones[:], mask_bf[:], start=True, stop=True).then_inc(ranks_ready, 1)
                elif what == "blocks":
                    pe.wait_ge(ended_ready, 1)
                    pe.matmul(pk[2][0:1, 0:BW], ones[0:E, 0:1], ended[:], start=True, stop=True).then_inc(ended_counted, 1)
                elif what == "lists":
                    for j in range(NB):
                        n = s * NB + j
                        from_pool = s * len(POOL_TILES) + sum(t <= j for t in POOL_TILES)
                        pe.wait_ge(hot_ready, 2 * (n + 1) - from_pool)
                        if by_pool(j):
                            pe.wait_ge(hot_pool_ready, from_pool)
                        pe.matmul(pk[7][:, s * BW:(s + 1) * BW], hot_q[:, n % RING], hot_blk[:, n % RING],
                                  start=(j == 0), stop=(j == NB - 1)).then_inc(hot_used, 1)
            pe.wait_ge(rows_ready, 1)
            slots = {}

            def head(m, i):
                count = 4 if m is not None else 1
                for stage, at in (("first", i), ("second", i - 4)):
                    if m is None and not 0 <= at < BLK:
                        continue
                    ap = block_slot[0:1, at:at + 1] if m is None else block_slot[0:1, ds(at, count)]
                    _, got = nc.values_load_multi_w_load_instructions(
                        ap, engines=(mybir.EngineType.PE,), min_val=NS, max_val=SL - 1,
                        skip_runtime_bounds_check_because="clamped when computed")
                    slots[stage] = got

            def turn(i, u, has, m):
                n = 0 if m is None else u - LEAD
                if m is None and i == -1:
                    pe.wait_ge(z_added, NB)
                if has(-2):
                    pe.wait_ge(gathered[(u + 2) % 4], 16 * ((i + 2) // 4 + 1 if m is None else m + (u + 2) // 4 + 1))
                    need(pe, FF["r", "xlo_ready"], i + 1)
                    x_turn("r", i, pk[u % 2], g_rows[:, (u + 2) % 4])
                if m is None and i == 0:
                    pe.wait_ge(wlo_ready, 2 * (SL - LAST))
                    pe.wait_ge(wlo_last, 2 * LAST)
                if has(0):
                    slot = slots["first"][n]
                    pe.wait_ge(FF["r", "xlo_ready"], i + 1)
                    need(pe, FF["r", "h_ready"], i - 1)
                    products(pk[4 + u % 2][:, 0:2 * I], lambda c: x_hi[:, u % 2, c], lambda c: x_lo[:, u % 2, c],
                             lambda c: w13_hi[:, ds(slot, 1), c], lambda c: w13_lo[:, ds(slot, 1), c]
                             ).then_inc(FF["r", "h13_ready"], 1)
                if has(4):
                    slot = slots["second"][n]
                    pe.wait_ge(FF["r", "hlo_ready"], i - 3)
                    need(pe, y_staged, i - 5)
                    products(YB[u % 2][:, 0:C], lambda c: h_hi[0:IH, u % 2, c], lambda c: h_lo[0:IH, u % 2, c],
                             lambda c: w2_hi[0:IH, ds(slot, 1), c], lambda c: w2_lo[0:IH, ds(slot, 1), c]
                             ).then_inc(FF["r", "y_ready"], 1)
                if has(2):
                    pe.wait_ge(FF["r", "h_ready"], i - 1)
                    need(pe, FF["r", "hlo_ready"], i - 3)
                    h_turn("r", (u + 2) % 4, HT[u % 2])

            run_blocks(pe, turn, head)

        @block.vector
        def _(dve):
            done = [0]

            def step(ins):
                done[0] += 1
                ins.then_inc(vstep, 1)
                return done[0]

            def after(n):
                dve.wait_ge(vstep, n)

            n = step(dve.memset(decay_row[:], 0.0))
            step(dve.memset(aa[:], 0.0))
            step(dve.memset(bb[:], 0.0))
            step(dve.memset(pp[0][:], NEG))
            step(dve.memset(pp[1][:], NEG))
            dve.wait_ge(decay_exp, 1)
            m = step(dve.tensor_scalar(wdec[:], wneg[:], -1.0, None, ALU.mult))
            step(dve.tensor_scalar(uneg[:], tf[:], -1.0, None, ALU.mult))
            dve.wait_ge(wg_split, 1)
            dve.tensor_tensor(wg_parts[:, :, E:2 * E], wg_raw[:], f32(wg_parts[:, :, 0:E]), ALU.subtract).then_inc(wg_split, 1)
            after(m)
            for hh in range(2):
                n = step(dve.tensor_scalar(decay_row[:, hh], decay_row[:, hh], wdec[:, hh:hh + 1], None, ALU.add))
            after(n)
            n = step(dve.memset(decay_row[:].rearrange("p h (b t) -> p h b t", t=P)[:, :, :, 0], NEG))
            after(n)

            def norm_stats(l, src, ready):
                for b in range(GB):
                    dve.bn_stats(stats[:, b], src(b)).then_inc(stats_ready, 1)
                counts[0] += GB
                dve.wait_ge(stats_ready, counts[0])
                for b in range(GB):
                    i = dve.bn_aggr(mv[l][:, b], stats[:, b])
                i.then_inc(ready, 1)

            counts = [0]

            def x_lo_part(kind, i, lo, hi, bank):
                dve.wait_ge(FF[kind, "xhi_ready"], i + 1)
                dve.tensor_tensor(lo.rearrange("p c t -> p (c t)"), bank[:, 0:2 * P],
                                  f32(hi).rearrange("p c t -> p (c t)"), ALU.subtract
                                  ).then_inc(FF[kind, "xlo_ready"], 1)

            def h_lo_part(kind, i, u, bank):
                dve.wait_ge(FF[kind, "hhi_ready"], i + 1)
                dve.tensor_tensor(h_lo[0:IH, u % 2].rearrange("p c t -> p (c t)"), bank[0:IH, 0:2 * P],
                                  f32(h_hi[0:IH, u % 2]).rearrange("p c t -> p (c t)"), ALU.subtract
                                  ).then_inc(FF[kind, "hlo_ready"], 1)

            mark = {}

            def ffn(n):
                u = n - 1
                if 0 <= u < UNITS:
                    dve.wait_ge(FF["s", "silu_ready"], u + 1)
                    bank = pk[4 + u % 2]
                    dve.scalar_tensor_tensor(h[:, u % 4], h[:, u % 4], 1.0, bank[:, 0:I], ALU.add, ALU.mult).then_inc(gated, 1)
                w = n - 3
                if 0 <= w < UNITS:
                    h_lo_part("s", w, w, HT[w % 2])
                if 0 <= u < UNITS:
                    dve.wait_ge(gated, u + 1)
                    dve.tensor_tensor(h[:, u % 4], h[:, u % 4], bank[:, I:2 * I], ALU.mult).then_inc(FF["s", "h_ready"], 1)
                if n >= 6 and n % 2 == 0:
                    add_z((n - 6) // 2)

            def add_z(t):
                dve.wait_ge(FF["s", "y_ready"], 2 * t + 2)
                dve.scalar_tensor_tensor(base[:, t], pk[1][:, 0:C], 0.5, base[:, t], ALU.mult, ALU.add).then_inc(z_added, 1)

            def recurrence(what, s):
                g = s // 2
                if what == "max":
                    dve.wait_ge(k_ready, s + 1)
                    need(dve, d_raw, s - 1)
                    dve.tensor_tensor_scan(pp[s % 2][:, 1:N + 1], decay_row[:, s % 2], k_c[s % 2][:], NEG,
                                           ALU.add, ALU.max).then_inc(pp_ready, 1)
                pos_, neg_, kv_ = clamp_pos[s % 2], clamp_neg[s % 2], kv[s % 2]
                if what == "sums":
                    dve.wait_ge(exp_ready, 2 * (s + 1))
                    mark["b"] = step(dve.tensor_tensor_scan(bb[:, 1:N + 1], neg_[:, 0], pos_[:, 0], 0.0, ALU.mult, ALU.add))
                    dve.wait_ge(kv_ready, s + 1)
                    mark["a"] = step(dve.tensor_tensor_scan(aa[:, 1:N + 1], neg_[:, 0], kv_[:, 0], 0.0, ALU.mult, ALU.add))
                elif what == "ratio":
                    after(mark["b"])
                    b2 = step(dve.tensor_tensor(den[:], neg_[:, 1], bb[:, 0:N], ALU.mult))
                    after(mark["a"])
                    need(dve, yT_ready, s - 1)
                    a2 = step(dve.tensor_tensor(num[s % 2][:], neg_[:, 1], aa[:, 0:N], ALU.mult))
                    after(b2)
                    mark["b"] = step(dve.tensor_tensor(den[:], den[:], pos_[:, 1], ALU.add))
                    after(a2)
                    dve.tensor_tensor(num[s % 2][:], num[s % 2][:], kv_[:, 1], ALU.add).then_inc(kv_used, 1)
                elif what == "recip":
                    after(mark["b"])
                    mark["b"] = step(dve.reciprocal(den[:], den[:]))
                elif what == "wkv":
                    after(mark["b"])
                    dve.wait_ge(kv_used, s + 1)
                    dve.tensor_tensor(num[s % 2][:], num[s % 2][:], den[:], ALU.mult).then_inc(wkv_ready, 1)
                elif what == "x1":
                    dve.wait_ge(yT_ready, s + 1)
                    cols = slice(s % 2 * P, (s % 2 + 1) * P)
                    dve.tensor_tensor(base[:, GB * g:GB * (g + 1), cols], pk[2][:].rearrange("p (b c) -> p b c", b=GB),
                                      x_in[:, g % 3, :, cols], ALU.add).then_inc(x1_ready, 1)

            def norms(what, g):
                if what == "ln1":
                    dve.wait_ge(x_loaded[g % 3], 16 * (g // 3 + 1))
                    need(dve, rstd1_ready, g)
                    norm_stats(0, lambda b: x_in[:, g % 3, b], mv1_ready)
                else:
                    dve.wait_ge(x1_ready, 2 * g + 2)
                    need(dve, rstd2_ready, g)
                    norm_stats(1, lambda b: base[:, GB * g + b], mv2_ready)

            def bc(ap, shape):
                return ap.broadcast_to(shape)

            def scores():
                dve.wait_ge(logits_copied, NB)
                n = step(dve.tensor_reduce(tmax[:], logits[:], AX.X, ALU.max))
                after(n)
                dve.tensor_tensor(masked[:], logits[:], bc(tmax[:].unsqueeze(2), [P, NB, E]), ALU.subtract).then_inc(shifted, 1)
                dve.wait_ge(scores_exp, 1)
                n = step(dve.tensor_reduce(tsum[:], score[:], AX.X, ALU.add))
                after(n)
                n = step(dve.reciprocal(trec[:], tsum[:]))
                after(n)
                n = step(dve.tensor_tensor(score[:], score[:], bc(trec[:].unsqueeze(2), [P, NB, E]), ALU.mult))
                after(n)
                n = step(dve.tensor_reduce(grp[:], score[:].rearrange("p j (g e) -> p (j g) e", g=NG), AX.X, ALU.max))
                after(n)
                gv = grp[:].rearrange("p (j g) -> p j g", g=NG)
                one = bc(gv.unsqueeze(3), [P, NB, NG, NG])
                other = bc(gv.unsqueeze(2), [P, NB, NG, NG])

                def v4(t):
                    return t[:].rearrange("p j (g h) -> p j g h", g=NG)
                step(dve.tensor_tensor(v4(cmp_gt), other, one, ALU.is_gt))
                n = step(dve.tensor_tensor(v4(cmp_eq), other, one, ALU.is_equal))
                after(n)
                n = step(dve.tensor_tensor(v4(cmp_eq), v4(cmp_eq), bc(lower[:].unsqueeze(1), [P, NB, NG, NG]), ALU.mult))
                after(n)
                n = step(dve.tensor_tensor(cmp_gt[:], cmp_gt[:], cmp_eq[:], ALU.add))
                after(n)
                n = step(dve.tensor_reduce(grank[:], cmp_gt[:].rearrange("p j (g h) -> p (j g) h", g=NG), AX.X, ALU.add))
                after(n)
                n = step(dve.tensor_scalar(gmask[:], grank[:], float(TOP_G), None, ALU.is_lt))
                after(n)
                gm = bc(gmask[:].unsqueeze(2), [P, NB * NG, GS])
                mk = masked[:].rearrange("p j (g e) -> p (j g) e", g=NG)
                n = step(dve.tensor_tensor(mk, score[:].rearrange("p j (g e) -> p (j g) e", g=NG), gm, ALU.mult))
                after(n)
                n = step(dve.scalar_tensor_tensor(mk, gm, -1.0, mk, ALU.add, ALU.add))
                after(n)

            def top_():
                for j in range(NB):
                    n = step(dve.max(topv[:, j], masked[:, j]))
                for j in range(NB):
                    after(n - NB + 1 + j)
                    m = step(dve.max_index(topi[:, j], topv[:, j], masked[:, j]))
                after(m)

            def mask():
                n = step(dve.tensor_copy(posk[:].rearrange("p (j k) -> p j k", k=TOP), topi[:, :, 0:TOP]))
                after(n)
                n = step(dve.tensor_tensor(onehot[:], bc(iota_row[:, 0:E].unsqueeze(1), [P, NB * TOP, E]),
                                           bc(posk[:].unsqueeze(2), [P, NB * TOP, E]), ALU.is_equal))
                after(n)
                oh = onehot[:].rearrange("p (j k) e -> p j e k", k=TOP)
                with nc.allow_low_precision(reason="counts of 0 or 1"):
                    dve.tensor_reduce(mask_bf[:].rearrange("p (j e) -> p j e", e=E), oh, AX.X, ALU.add).then_inc(mask_ready, 1)

            def ranks():
                n = step(dve.memset(reset[:], 1.0))
                after(n)
                step(dve.memset(reset[:, :, 0], 0.0))
                dve.wait_ge(ranks_ready, 1)
                n = step(dve.tensor_copy(total[:], pk[2][:, 0:NB * E].rearrange("p (j e) -> p e j", e=E)))
                after(n)
                flat = "p e j -> p (e j)"
                n = step(dve.tensor_tensor_scan(cmp_gt[:].rearrange(flat), reset[:].rearrange(flat), total[:].rearrange(flat), 0.0,
                                                ALU.mult, ALU.add))
                after(n)

            def blocks():
                counts_ = cmp_gt[:][:, :, NB - 1]
                n = step(dve.tensor_tensor(cmp_eq[:], bc(counts_.unsqueeze(2), [P, E, NB]),
                                           bc(steps[:].unsqueeze(1), [P, E, NB]), ALU.is_gt))
                after(n)
                n = step(dve.tensor_reduce(nblk[:], cmp_eq[:], AX.X, ALU.add))
                after(n)
                n = step(dve.tensor_tensor_scan(bend[:], ones[:, 0:E], nblk[:], 0.0, ALU.mult, ALU.add))
                after(n)
                n = step(dve.tensor_tensor(bstart[:], bend[:], nblk[:], ALU.subtract))
                m = step(dve.tensor_tensor(tmax[:], bend[:], ident[:, 0:E], ALU.mult))
                after(m)
                m = step(dve.tensor_reduce(bend_of[:], tmax[:], AX.X, ALU.add))
                after(m)
                dve.tensor_scalar(ended[:], iota_row[0:E, 0:BW], bend_of[0:E], None, ALU.is_ge).then_inc(ended_ready, 1)

            def places():
                m = step(dve.tensor_tensor(cmp_gt[:], cmp_gt[:], total[:], ALU.subtract))
                after(m)
                m = step(dve.tensor_tensor(pos[:], pk[0][:, 0:NB * E].rearrange("p (j e) -> p j e", e=E),
                                           cmp_gt[:].rearrange("p e j -> p j e"), ALU.add))
                after(m)
                m = step(dve.scalar_tensor_tensor(pos[:], bc(bstart[:].unsqueeze(1), [P, NB, E]), float(P), pos[:], ALU.mult, ALU.add))
                after(m)
                m = step(dve.tensor_tensor(picked[:].rearrange("p (j k) e -> p j k e", k=TOP),
                                           onehot[:].rearrange("p (j k) e -> p j k e", k=TOP),
                                           bc(pos[:].unsqueeze(2), [P, NB, TOP, E]), ALU.mult))
                after(m)
                m = step(dve.tensor_reduce(posk[:], picked[:], AX.X, ALU.add))
                after(m)
                m = step(dve.tensor_copy(posi[:], posk[:]))
                after(m)
                step(dve.tensor_scalar(blki[:], posi[:], 7, None, ALU.arith_shift_right))
                m = step(dve.tensor_scalar(placei[:], posi[:], P - 1, None, ALU.bitwise_and))
                after(m)
                step(dve.tensor_copy(blkf[:], blki[:]))
                m = step(dve.tensor_copy(placef[:], placei[:]))
                after(m)
                dve.sem_inc(places_ready, 1)
                dve.wait_ge(ended_counted, 1)
                m = step(dve.tensor_scalar(slotf[:], pk[2][0:1, 0:BW], float(E - 1), float(NS), ALU.min, ALU.add))
                after(m)
                step(dve.tensor_copy(block_slot[:], slotf[:]))

            def lists(k):
                for j in range(NB):
                    n = k * NB + j
                    at = j * TOP + k
                    need(dve, hot_used, n - RING + 1)
                    dve.tensor_scalar(hot_q[:, n % RING], iota_row[:], placef[:, at:at + 1], None, ALU.is_equal
                                      ).then_inc(hot_ready, 1)
                    if not by_pool(j):
                        dve.tensor_scalar(hot_blk[:, n % RING], iota_row[:, 0:BW], blkf[:, at:at + 1], token_1[:, j:j + 1],
                                          ALU.is_equal, ALU.mult).then_inc(hot_ready, 1)

            def rows():
                dve.wait_ge(hot_used, NB * TOP)
                n = step(dve.tensor_copy(listed[:].rearrange("p k b -> p (k b)"), pk[7][:, 0:TOP * BW]))
                after(n)
                step(dve.tensor_scalar(filled[:], listed[:], 0.5, None, ALU.is_gt))
                n = step(dve.tensor_reduce(tok[:], listed[:].rearrange("p k b -> p b k"), AX.X, ALU.add))
                after(n)
                a1 = step(dve.scalar_tensor_tensor(kth[:], filled[:, 2], 2.0, filled[:, 1], ALU.mult, ALU.add))
                step(dve.tensor_scalar(empty[:], tok[:], 0.5, PAD, ALU.is_lt, ALU.mult))
                a2 = step(dve.tensor_scalar(rows_f[:], tok[:], -1.0, 0.0, ALU.add, ALU.max))
                after(a2)
                a2 = step(dve.tensor_copy(rows_in[:], rows_f[:]))
                after(a1)
                a1 = step(dve.scalar_tensor_tensor(kth[:], filled[:, 3], 3.0, kth[:], ALU.mult, ALU.add))
                after(a1)
                a1 = step(dve.scalar_tensor_tensor(kth[:], kth[:], float(NT), tok[:], ALU.mult, ALU.add))
                after(a1)
                a1 = step(dve.scalar_tensor_tensor(kth[:], kth[:], -1.0, empty[:], ALU.add, ALU.add))
                after(a1)
                a1 = step(dve.tensor_copy(rows_out[:], kth[:]))
                after(a1)
                dve.sem_inc(rows_ready, 1)

            for what, *a in order:
                if what in ("ln1", "ln2"):
                    norms(what, a[0])
                elif what == "low":
                    g, b = a
                    x_lo_part("s", GB * g + b, s_x_lo[:, b], s_x_hi[:, b], x_bank(g, b))
                elif what == "gather":
                    g = a[0]
                    dve.wait_ge(logits_ready, GB * (g + 1))
                    parts = pk[7][:, 2 * P:2 * P + GB * 2 * E].rearrange("p (b h e) -> p b h e", h=2, e=E)
                    n = step(dve.tensor_copy(logits[:, GB * g:GB * (g + 1)], parts[:, :, 0]))
                    after(n)
                    dve.tensor_tensor(logits[:, GB * g:GB * (g + 1)], logits[:, GB * g:GB * (g + 1)], parts[:, :, 1],
                                      ALU.add).then_inc(logits_copied, GB)
                elif what == "ffn":
                    ffn(a[0])
                elif what == "lists":
                    lists(a[0])
                    if a[0] == TOP - 1:
                        rows()
                elif what == "scores":
                    scores()
                elif what == "top":
                    top_()
                elif what == "mask":
                    mask()
                elif what == "ranks":
                    ranks()
                elif what == "blocks":
                    blocks()
                elif what == "places":
                    places()
                elif what not in ("kt", "key", "clamp", "kv", "xhat", "split", "turn", "logits", "back"):
                    recurrence(what, a[0])
            for slot in range(SL - LAST, SL):
                dve.wait_ge(whi_ready, 2 * (slot + 1))
                dve.tensor_tensor(w13_lo[:, slot], w13_raw[:, slot], f32(w13_hi[:, slot]), ALU.subtract).then_inc(wlo_last, 1)
                dve.tensor_tensor(w2_lo[0:IH, slot], w2_raw[0:IH, slot], f32(w2_hi[0:IH, slot]), ALU.subtract).then_inc(wlo_last, 1)
            add_z(NB - 1)

            def turn(i, u, has, m):
                if has(-1):
                    x_lo_part("r", i + 1, x_lo[:, (u + 1) % 2], x_hi[:, (u + 1) % 2], pk[(u + 1) % 2])
                if has(1):
                    dve.wait_ge(FF["r", "silu_ready"], i)
                    dve.tensor_tensor(h[:, (u - 1) % 4], h[:, (u - 1) % 4], pk[4 + (u - 1) % 2][:, I:2 * I], ALU.mult
                                      ).then_inc(FF["r", "h_ready"], 1)
                if has(3):
                    h_lo_part("r", i - 3, u - 3, HT[(u - 3) % 2])

            run_blocks(dve, turn)
            dve.wait_ge(z_added, NB)
            last = {}
            for n_ in range(NB // 2):
                for k in range(TOP):
                    dve.wait_ge(pairs_loaded[n_][k], 16)
                    for j in (2 * n_, 2 * n_ + 1):
                        if k:
                            after(last[j])
                        i = dve.scalar_tensor_tensor(base[:, j], pairs_in[:, k, j], topv[:, j, k:k + 1], base[:, j],
                                                     ALU.mult, ALU.add)
                        if k == TOP - 1:
                            i.then_inc(summed, 1)
                        else:
                            last[j] = step(i)


_INS = ["x", "ctx", "decay", "first", "wg", "w13", "w2"]


def kernel(x, ctx_2048, L0_xattn_time_decay, L0_xattn_time_first, L0_ffn_Wg, L0_ffn_W1, L0_ffn_W3, L0_ffn_W2,
           L0_ffn_Ws1, L0_ffn_Ws3, L0_ffn_Ws2):
    import concourse.bacc as _bacc
    from concourse.bass_utils import run_bass_kernel_spmd as _run

    a = {k: np.asarray(t) for k, t in dict(x=x, ctx=ctx_2048, decay=L0_xattn_time_decay, first=L0_xattn_time_first,
                                           wg=L0_ffn_Wg, w1=L0_ffn_W1, w3=L0_ffn_W3, w2=L0_ffn_W2, s1=L0_ffn_Ws1,
                                           s3=L0_ffn_Ws3, s2=L0_ffn_Ws2).items()}
    w1 = np.concatenate([a["s1"].reshape(NS, I, C), a["w1"]])
    w3 = np.concatenate([a["s3"].reshape(NS, I, C), a["w3"]])
    w2 = np.concatenate([a["s2"].reshape(C, NS, I).transpose(1, 0, 2), a["w2"]])
    w13 = np.concatenate([w1, w3], axis=1)
    arrays = {
        "x": a["x"],
        "ctx": a["ctx"].reshape(G, GB, P, 2, P).transpose(4, 0, 3, 1, 2).reshape(P, G, 2, N),
        "decay": a["decay"].reshape(2, P).T, "first": a["first"].reshape(2, P).T,
        "wg": a["wg"].reshape(E, 2, P).transpose(2, 1, 0),
        "w13": w13.reshape(NS + E, 2 * I, 2, P).transpose(3, 0, 2, 1),
        "w2": w2.reshape(NS + E, C, 2, IH).transpose(3, 0, 2, 1),
    }
    nc = _bacc.Bacc("TRN2", target_bir_lowering=False, num_devices=1)
    data, args = {}, []
    for name in _INS:
        t = np.ascontiguousarray(arrays[name])
        data[f"in_{name}_dram"] = t
        args.append(nc.dram_tensor(f"in_{name}_dram", t.shape, mybir.dt.from_np(t.dtype), kind="ExternalInput").ap())
    o = nc.dram_tensor("out_0_dram", (NB, P, C), F32, kind="ExternalOutput").ap()
    xattn_moe_kernel(nc, *args, o)
    r = _run(nc, [data], core_ids=[0])
    return r.results[0]["out_0_dram"]
```
